# Optimizing a Trainium2 kernel written in Bass

```python
import numpy as np
import jax
import jax.numpy as jnp

def _softmax(x, axis=-1):
    return jax.nn.softmax(x, axis=axis)

def _gelu(x):
    return jax.nn.gelu(x, approximate=True)

def _silu(x):
    return jax.nn.silu(x)

def _sigmoid(x):
    return jax.nn.sigmoid(x)

def _layernorm(x, axis=-1, eps=1e-05):
    m = jnp.mean(x, axis=axis, keepdims=True)
    v = jnp.var(x, axis=axis, keepdims=True)
    return (x - m) / jnp.sqrt(v + eps)

def _scatter_add(tgt, idx, src, axis=0):
    return tgt.at[idx].add(src)

def _segment_sum(src, seg, n):
    return jax.ops.segment_sum(src, seg, n)
kernel_name = 'mk_cond_seq_d4_seqx_r8_1e5165'

def setup_inputs(seed: int=0):
    np.random.seed(seed)
    _w = jnp.asarray

    def _rec_inputs():
        import jax
        import jax.numpy as jnp
        _rk = jax.random.key(seed)
        x = 1.648e-05 + 1 * jax.random.normal(jax.random.fold_in(_rk, 1), (2, 512, 144), jnp.float32)
        _lenS = 512 - jax.random.randint(jax.random.fold_in(_rk, 7), (2,), 0, max(1, 512 // 4) + 1, jnp.int32)
        _lenS2 = 512 - jax.random.randint(jax.random.fold_in(_rk, 8), (2,), 0, max(1, 512 // 4) + 1, jnp.int32)
        cond_1152 = 0.00914911 + 1.00357 * jax.random.normal(jax.random.fold_in(_rk, 11), (2, 144), jnp.float32)
        return (x, cond_1152)
    x, cond_1152 = _rec_inputs()

    def _L0_cond_setup():
        import jax, jax.numpy as jnp
        import numpy as np
        NUM_HEADS = 16
        NUM_EXPERTS = 4
        TOP_K = 2
        LN_EPS = 1e-06

        def _ln(h):
            mu = jnp.mean(h, axis=-1, keepdims=True)
            var = jnp.var(h, axis=-1, keepdims=True)
            return (h - mu) * jax.lax.rsqrt(var + LN_EPS)

        def _modulate(h, shift, scale):
            return h * (1.0 + scale[:, None, :]) + shift[:, None, :]
        key = jax.random.key(seed)
        ks = jax.random.split(key, 12)
        B, N, C = (8, 128, 144)
        H = 4 * C
        E = NUM_EXPERTS
        s = 0.02
        return {'x': jax.random.normal(ks[0], (B, N, C), jnp.float32), 'c': jax.random.normal(ks[1], (B, C), jnp.float32), 'w_adaln': jax.random.normal(ks[2], (C, 6 * C), jnp.float32) * s, 'b_adaln': jnp.zeros((6 * C,), jnp.float32), 'w_qkv': jax.random.normal(ks[3], (C, 3 * C), jnp.float32) * s, 'b_qkv': jnp.zeros((3 * C,), jnp.float32), 'w_proj': jax.random.normal(ks[4], (C, C), jnp.float32) * s, 'b_proj': jnp.zeros((C,), jnp.float32), 'w_gate': jax.random.normal(ks[5], (C, E), jnp.float32) * s, 'w1': jax.random.normal(ks[6], (E, C, H), jnp.float32) * s, 'b1': jnp.zeros((E, H), jnp.float32), 'w2': jax.random.normal(ks[7], (E, H, C), jnp.float32) * s, 'b2': jnp.zeros((E, C), jnp.float32)}
    _L0_cond_all = _L0_cond_setup()
    _L0_cond_in = {k: v for k, v in _L0_cond_all.items() if k in ('w_adaln', 'b_adaln', 'w_qkv', 'b_qkv', 'w_proj', 'b_proj', 'w_gate', 'w1', 'b1', 'w2', 'b2')}
    del _L0_cond_all

    def _L1_cond_setup():
        import jax, jax.numpy as jnp
        import numpy as np
        H = 144
        NH = 16
        HD = H // NH
        MLP = int(H * 4.0)
        EPS = 1e-06

        def _ln(z, scale=None):
            m = jnp.mean(z, axis=-1, keepdims=True)
            v = jnp.mean(jnp.square(z - m), axis=-1, keepdims=True)
            y = (z - m) * jax.lax.rsqrt(v + EPS)
            if scale is not None:
                y = y * scale
            return y
        key = jax.random.key(seed)
        ks = jax.random.split(key, 16)
        B, N = (16, 128)
        x = jax.random.normal(ks[0], (B, N, H), dtype=jnp.float32)
        c = jax.random.normal(ks[1], (B, H), dtype=jnp.float32)

        def xav(k, fan_in, fan_out):
            lim = np.sqrt(6.0 / (fan_in + fan_out))
            return jax.random.uniform(k, (fan_in, fan_out), jnp.float32, -lim, lim)
        w_mod = 0.02 * jax.random.normal(ks[2], (H, 6 * H), dtype=jnp.float32)
        b_mod = 0.02 * jax.random.normal(ks[3], (6 * H,), dtype=jnp.float32)
        w_qkv = xav(ks[4], H, 3 * H)
        b_qkv = jnp.zeros((3 * H,), jnp.float32)
        g_q = jnp.ones((HD,), jnp.float32)
        g_k = jnp.ones((HD,), jnp.float32)
        w_proj = xav(ks[5], H, H)
        b_proj = jnp.zeros((H,), jnp.float32)
        w1 = xav(ks[6], H, MLP)
        b1 = jnp.zeros((MLP,), jnp.float32)
        w2 = xav(ks[7], MLP, H)
        b2 = jnp.zeros((H,), jnp.float32)
        return dict(x=x, c=c, w_mod=w_mod, b_mod=b_mod, w_qkv=w_qkv, b_qkv=b_qkv, g_q=g_q, g_k=g_k, w_proj=w_proj, b_proj=b_proj, w1=w1, b1=b1, w2=w2, b2=b2)
    _L1_cond_all = _L1_cond_setup()
    _L1_cond_in = {k: v for k, v in _L1_cond_all.items() if k in ('w_mod', 'b_mod', 'w_qkv', 'b_qkv', 'g_q', 'g_k', 'w_proj', 'b_proj', 'w1', 'b1', 'w2', 'b2')}
    del _L1_cond_all

    def _L2_cond_setup():
        import jax, jax.numpy as jnp
        import numpy as np
        B, L, C = (8, 128, 144)
        H = 16
        D = C // H
        FF = int(C * 4.0)
        EPS = 1e-06

        def _layernorm(x):
            mu = jnp.mean(x, axis=-1, keepdims=True)
            var = jnp.mean(jnp.square(x - mu), axis=-1, keepdims=True)
            return (x - mu) * jax.lax.rsqrt(var + EPS)

        def _modulate(x, shift, scale):
            return x * (1.0 + scale) + shift

        def _attention(h, W_qkv, b_qkv, W_proj, b_proj):
            b, l, c = h.shape
            qkv = h @ W_qkv + b_qkv
            qkv = qkv.reshape(b, l, 3, H, D)
            q, k, v = (qkv[:, :, 0], qkv[:, :, 1], qkv[:, :, 2])
            scale = D ** (-0.5)
            scores = jnp.einsum('blhd,bmhd->bhlm', q * scale, k)
            attn = jax.nn.softmax(scores, axis=-1)
            o = jnp.einsum('bhlm,bmhd->blhd', attn, v).reshape(b, l, c)
            return o @ W_proj + b_proj
        key = jax.random.key(seed)
        ks = jax.random.split(key, 12)
        s = 0.02
        return {'x': jax.random.normal(ks[0], (B, L, C), jnp.float32), 'c': jax.random.normal(ks[1], (B, 1, C), jnp.float32), 'W_qkv': jax.random.normal(ks[2], (C, 3 * C), jnp.float32) * s, 'b_qkv': jnp.zeros((3 * C,), jnp.float32), 'W_proj': jax.random.normal(ks[3], (C, C), jnp.float32) * s, 'b_proj': jnp.zeros((C,), jnp.float32), 'W_fc1': jax.random.normal(ks[4], (C, FF), jnp.float32) * s, 'b_fc1': jnp.zeros((FF,), jnp.float32), 'W_fc2': jax.random.normal(ks[5], (FF, C), jnp.float32) * s, 'b_fc2': jnp.zeros((C,), jnp.float32), 'W_ada': jax.random.normal(ks[6], (C, 6 * C), jnp.float32) * s, 'b_ada': jnp.zeros((6 * C,), jnp.float32)}
    _L2_cond_all = _L2_cond_setup()
    _L2_cond_in = {k: v for k, v in _L2_cond_all.items() if k in ('W_qkv', 'b_qkv', 'W_proj', 'b_proj', 'W_fc1', 'b_fc1', 'W_fc2', 'b_fc2', 'W_ada', 'b_ada')}
    del _L2_cond_all

    def _L3_cond_setup():
        import jax, jax.numpy as jnp
        import numpy as np
        from jax.scipy.linalg import expm
        N, D, COND_DIM = (144, 64, 144)
        B, T = (16, 128)

        def _rotation(cond, W, b):
            v = jax.nn.silu(cond) @ W.T + b
            iu, ju = jnp.triu_indices(D, k=1)
            A = jnp.zeros((cond.shape[0], D, D), dtype=v.dtype)
            A = A.at[:, iu, ju].set(v).at[:, ju, iu].set(-v)
            return expm(A)
        key = jax.random.key(seed)
        k1, k2, k3, k4, k5 = jax.random.split(key, 5)
        x = jax.random.normal(k1, (B, T, N), dtype=jnp.float32)
        cond = jax.random.normal(k2, (B, COND_DIM), dtype=jnp.float32)
        P = jax.random.normal(k3, (N, D), dtype=jnp.float32)
        n_skew = D * (D - 1) // 2
        bound = 1.0 / np.sqrt(COND_DIM)
        W = jax.random.uniform(k4, (n_skew, COND_DIM), minval=-bound, maxval=bound, dtype=jnp.float32)
        b = jax.random.uniform(k5, (n_skew,), minval=-bound, maxval=bound, dtype=jnp.float32)
        return {'x': x, 'cond': cond, 'P': P, 'W': W, 'b': b}
    _L3_cond_all = _L3_cond_setup()
    _L3_cond_in = {k: v for k, v in _L3_cond_all.items() if k in ('P', 'W', 'b')}
    del _L3_cond_all
    return {'x': x, 'cond_1152': cond_1152, 'L0_cond_w_adaln': _L0_cond_in['w_adaln'], 'L0_cond_b_adaln': _L0_cond_in['b_adaln'], 'L0_cond_w_qkv': _L0_cond_in['w_qkv'], 'L0_cond_b_qkv': _L0_cond_in['b_qkv'], 'L0_cond_w_proj': _L0_cond_in['w_proj'], 'L0_cond_b_proj': _L0_cond_in['b_proj'], 'L0_cond_w_gate': _L0_cond_in['w_gate'], 'L0_cond_w1': _L0_cond_in['w1'], 'L0_cond_b1': _L0_cond_in['b1'], 'L0_cond_w2': _L0_cond_in['w2'], 'L0_cond_b2': _L0_cond_in['b2'], 'L1_cond_w_mod': _L1_cond_in['w_mod'], 'L1_cond_b_mod': _L1_cond_in['b_mod'], 'L1_cond_w_qkv': _L1_cond_in['w_qkv'], 'L1_cond_b_qkv': _L1_cond_in['b_qkv'], 'L1_cond_g_q': _L1_cond_in['g_q'], 'L1_cond_g_k': _L1_cond_in['g_k'], 'L1_cond_w_proj': _L1_cond_in['w_proj'], 'L1_cond_b_proj': _L1_cond_in['b_proj'], 'L1_cond_w1': _L1_cond_in['w1'], 'L1_cond_b1': _L1_cond_in['b1'], 'L1_cond_w2': _L1_cond_in['w2'], 'L1_cond_b2': _L1_cond_in['b2'], 'L2_cond_W_qkv': _L2_cond_in['W_qkv'], 'L2_cond_b_qkv': _L2_cond_in['b_qkv'], 'L2_cond_W_proj': _L2_cond_in['W_proj'], 'L2_cond_b_proj': _L2_cond_in['b_proj'], 'L2_cond_W_fc1': _L2_cond_in['W_fc1'], 'L2_cond_b_fc1': _L2_cond_in['b_fc1'], 'L2_cond_W_fc2': _L2_cond_in['W_fc2'], 'L2_cond_b_fc2': _L2_cond_in['b_fc2'], 'L2_cond_W_ada': _L2_cond_in['W_ada'], 'L2_cond_b_ada': _L2_cond_in['b_ada'], 'L3_cond_P': _L3_cond_in['P'], 'L3_cond_W': _L3_cond_in['W'], 'L3_cond_b': _L3_cond_in['b']}

def reference(x, cond_1152, L0_cond_w_adaln, L0_cond_b_adaln, L0_cond_w_qkv, L0_cond_b_qkv, L0_cond_w_proj, L0_cond_b_proj, L0_cond_w_gate, L0_cond_w1, L0_cond_b1, L0_cond_w2, L0_cond_b2, L1_cond_w_mod, L1_cond_b_mod, L1_cond_w_qkv, L1_cond_b_qkv, L1_cond_g_q, L1_cond_g_k, L1_cond_w_proj, L1_cond_b_proj, L1_cond_w1, L1_cond_b1, L1_cond_w2, L1_cond_b2, L2_cond_W_qkv, L2_cond_b_qkv, L2_cond_W_proj, L2_cond_b_proj, L2_cond_W_fc1, L2_cond_b_fc1, L2_cond_W_fc2, L2_cond_b_fc2, L2_cond_W_ada, L2_cond_b_ada, L3_cond_P, L3_cond_W, L3_cond_b):
    import jax
    import jax.numpy as jnp

    def _L0_cond_ref(x, c, w_adaln, b_adaln, w_qkv, b_qkv, w_proj, b_proj, w_gate, w1, b1, w2, b2):
        import jax, jax.numpy as jnp
        import numpy as np
        NUM_HEADS = 16
        NUM_EXPERTS = 4
        TOP_K = 2
        LN_EPS = 1e-06

        def _ln(h):
            mu = jnp.mean(h, axis=-1, keepdims=True)
            var = jnp.var(h, axis=-1, keepdims=True)
            return (h - mu) * jax.lax.rsqrt(var + LN_EPS)

        def _modulate(h, shift, scale):
            return h * (1.0 + scale[:, None, :]) + shift[:, None, :]
        B, N, C = x.shape
        nh = NUM_HEADS
        hd = C // nh
        mod = jax.nn.silu(c) @ w_adaln + b_adaln
        sh_msa, sc_msa, g_msa, sh_mlp, sc_mlp, g_mlp = jnp.split(mod, 6, axis=-1)
        h = _modulate(_ln(x), sh_msa, sc_msa)
        qkv = (h @ w_qkv + b_qkv).reshape(B, N, 3, nh, hd).transpose(2, 0, 3, 1, 4)
        q, k, v = (qkv[0], qkv[1], qkv[2])
        attn = jax.nn.softmax(jnp.einsum('bhqd,bhkd->bhqk', q, k) * hd ** (-0.5), axis=-1)
        o = jnp.einsum('bhqk,bhkd->bhqd', attn, v).transpose(0, 2, 1, 3).reshape(B, N, C)
        o = o @ w_proj + b_proj
        x = x + g_msa[:, None, :] * o
        xn = _modulate(_ln(x), sh_mlp, sc_mlp)
        xf = xn.reshape(-1, C)
        gate_logits = xf @ w_gate
        topk_logits, topk_idx = jax.lax.top_k(gate_logits, TOP_K)
        gates = jax.nn.softmax(topk_logits, axis=-1)
        cw = jnp.sum(jax.nn.one_hot(topk_idx, NUM_EXPERTS, dtype=xf.dtype) * gates[..., None], axis=1)
        hmid = jax.nn.gelu(jnp.einsum('tc,ech->eth', xf, w1) + b1[:, None, :], approximate=True)
        eo = jnp.einsum('eth,ehc->etc', hmid, w2) + b2[:, None, :]
        moe = jnp.einsum('te,etc->tc', cw, eo).reshape(B, N, C)
        return x + g_mlp[:, None, :] * moe

    def _L1_cond_ref(x, c, w_mod, b_mod, w_qkv, b_qkv, g_q, g_k, w_proj, b_proj, w1, b1, w2, b2):
        import jax, jax.numpy as jnp
        import numpy as np
        H = 144
        NH = 16
        HD = H // NH
        MLP = int(H * 4.0)
        EPS = 1e-06

        def _ln(z, scale=None):
            m = jnp.mean(z, axis=-1, keepdims=True)
            v = jnp.mean(jnp.square(z - m), axis=-1, keepdims=True)
            y = (z - m) * jax.lax.rsqrt(v + EPS)
            if scale is not None:
                y = y * scale
            return y
        B, N, _ = x.shape
        mod = jax.nn.swish(c) @ w_mod + b_mod
        sh_msa, sc_msa, g_msa, sh_mlp, sc_mlp, g_mlp = jnp.split(mod, 6, axis=1)
        xn = _ln(x) * (1 + sc_msa[:, None, :]) + sh_msa[:, None, :]
        qkv = xn @ w_qkv + b_qkv
        qkv = qkv.reshape(B, N, 3, NH, HD).transpose(2, 0, 3, 1, 4)
        q, k, v = (qkv[0], qkv[1], qkv[2])
        q = _ln(q, g_q)
        k = _ln(k, g_k)
        attn = jax.nn.softmax(jnp.einsum('bhqd,bhkd->bhqk', q, k) * HD ** (-0.5), axis=-1)
        o = jnp.einsum('bhqk,bhkd->bhqd', attn, v)
        o = o.transpose(0, 2, 1, 3).reshape(B, N, H) @ w_proj + b_proj
        x = x + g_msa[:, None, :] * o
        xn2 = _ln(x) * (1 + sc_mlp[:, None, :]) + sh_mlp[:, None, :]
        h = jax.nn.gelu(xn2 @ w1 + b1, approximate=True)
        x = x + g_mlp[:, None, :] * (h @ w2 + b2)
        return x

    def _L2_cond_ref(x, c, W_qkv, b_qkv, W_proj, b_proj, W_fc1, b_fc1, W_fc2, b_fc2, W_ada, b_ada):
        import jax, jax.numpy as jnp
        import numpy as np
        B, L, C = (8, 128, 144)
        H = 16
        D = C // H
        FF = int(C * 4.0)
        EPS = 1e-06

        def _layernorm(x):
            mu = jnp.mean(x, axis=-1, keepdims=True)
            var = jnp.mean(jnp.square(x - mu), axis=-1, keepdims=True)
            return (x - mu) * jax.lax.rsqrt(var + EPS)

        def _modulate(x, shift, scale):
            return x * (1.0 + scale) + shift

        def _attention(h, W_qkv, b_qkv, W_proj, b_proj):
            b, l, c = h.shape
            qkv = h @ W_qkv + b_qkv
            qkv = qkv.reshape(b, l, 3, H, D)
            q, k, v = (qkv[:, :, 0], qkv[:, :, 1], qkv[:, :, 2])
            scale = D ** (-0.5)
            scores = jnp.einsum('blhd,bmhd->bhlm', q * scale, k)
            attn = jax.nn.softmax(scores, axis=-1)
            o = jnp.einsum('bhlm,bmhd->blhd', attn, v).reshape(b, l, c)
            return o @ W_proj + b_proj
        ada = jax.nn.silu(c) @ W_ada + b_ada
        shift_msa, scale_msa, gate_msa, shift_mlp, scale_mlp, gate_mlp = jnp.split(ada, 6, axis=-1)
        h = _modulate(_layernorm(x), shift_msa, scale_msa)
        x = x + gate_msa * _attention(h, W_qkv, b_qkv, W_proj, b_proj)
        h = _modulate(_layernorm(x), shift_mlp, scale_mlp)
        mlp = jax.nn.gelu(h @ W_fc1 + b_fc1, approximate=True) @ W_fc2 + b_fc2
        x = x + gate_mlp * mlp
        return x

    def _L3_cond_ref(x, cond, P, W, b):
        import jax, jax.numpy as jnp
        import numpy as np
        from jax.scipy.linalg import expm
        N, D, COND_DIM = (144, 64, 144)
        B, T = (16, 128)

        def _rotation(cond, W, b):
            v = jax.nn.silu(cond) @ W.T + b
            iu, ju = jnp.triu_indices(D, k=1)
            A = jnp.zeros((cond.shape[0], D, D), dtype=v.dtype)
            A = A.at[:, iu, ju].set(v).at[:, ju, iu].set(-v)
            return expm(A)
        U, _ = jnp.linalg.qr(P)
        R = _rotation(cond, W, b)
        z = jnp.einsum('btn,nd->btd', x, U)
        z_rot = jnp.einsum('btd,bde->bte', z, R)
        x_rot = x + jnp.einsum('btd,nd->btn', z_rot - z, U)
        return x_rot
    x = _L0_cond_ref(x, cond_1152, L0_cond_w_adaln, L0_cond_b_adaln, L0_cond_w_qkv, L0_cond_b_qkv, L0_cond_w_proj, L0_cond_b_proj, L0_cond_w_gate, L0_cond_w1, L0_cond_b1, L0_cond_w2, L0_cond_b2)
    x = _L1_cond_ref(x, cond_1152, L1_cond_w_mod, L1_cond_b_mod, L1_cond_w_qkv, L1_cond_b_qkv, L1_cond_g_q, L1_cond_g_k, L1_cond_w_proj, L1_cond_b_proj, L1_cond_w1, L1_cond_b1, L1_cond_w2, L1_cond_b2)
    x = _L2_cond_ref(x, cond_1152[:, None, :], L2_cond_W_qkv, L2_cond_b_qkv, L2_cond_W_proj, L2_cond_b_proj, L2_cond_W_fc1, L2_cond_b_fc1, L2_cond_W_fc2, L2_cond_b_fc2, L2_cond_W_ada, L2_cond_b_ada)
    x = _L3_cond_ref(x, cond_1152, L3_cond_P, L3_cond_W, L3_cond_b)
    return x

_drawn_inputs = setup_inputs


def setup_inputs(seed=0):
    import zlib

    import numpy as np

    out = dict(_drawn_inputs(seed))
    spreads = {'L0_cond_b_adaln': (0.0, 0.538),
     'L0_cond_b_qkv': (0.0, 0.8),
     'L0_cond_b_proj': (0.0, 0.431),
     'L0_cond_b1': (0.0, 0.8),
     'L0_cond_b2': (0.0, 0.705),
     'L1_cond_b_qkv': (0.0, 2.0),
     'L1_cond_g_q': (1.0, 0.6),
     'L1_cond_g_k': (1.0, 0.6),
     'L1_cond_b_proj': (0.0, 1.964),
     'L1_cond_b1': (0.0, 2.0),
     'L1_cond_b2': (0.0, 1.922),
     'L2_cond_b_qkv': (0.0, 0.8),
     'L2_cond_b_proj': (0.0, 0.433),
     'L2_cond_b_fc1': (0.0, 0.8),
     'L2_cond_b_fc2': (0.0, 0.478),
     'L2_cond_b_ada': (0.0, 0.486)}
    factors = {'L0_cond_w_adaln': 3.024,
     'L0_cond_w_qkv': 8.0,
     'L0_cond_w_proj': 8.0,
     'L0_cond_w_gate': 5.679,
     'L0_cond_w1': 7.253,
     'L0_cond_w2': 6.6,
     'L1_cond_b_mod': 5.096,
     'L1_cond_w_qkv': 2.978,
     'L2_cond_W_qkv': 8.0,
     'L2_cond_W_proj': 8.0,
     'L2_cond_W_fc1': 5.212,
     'L2_cond_W_fc2': 4.821}
    for name, (base, spread) in spreads.items():
        noise = np.random.default_rng([zlib.crc32(name.encode()), seed]).standard_normal(out[name].shape)
        drawn = base * np.exp(spread * noise) if base else spread * noise
        out[name] = jnp.asarray(drawn.astype(out[name].dtype))
    for name, factor in factors.items():
        out[name] = (out[name] * factor).astype(out[name].dtype)
    return out
```

```python
from contextlib import ExitStack

import concourse.bass as bass
from concourse import mybir

F32 = mybir.dt.float32
F32R = mybir.dt.float32r
I32 = mybir.dt.int32
ALU = mybir.AluOpType
ACT = mybir.ActivationFunctionType
AX = mybir.AxisListType
RMAX = bass.bass_isa.ReduceOp.max

P = 128
B, N, C = 2, 512, 144
NH, HD = 16, 9
T = N // P
CR = C - P
LAYERS, EXPERTS, TOP_K = 3, 4, 2
FF = 4 * C
FT = FF // P
FR = FF - FT * P
DW = 96
EPS = 1e-6
GRP = 4
G = NH // GRP
PROBS = 8
MAXROW = 3 * HD
VW = HD + 1
BLOCKS = LAYERS * B
UNITS = 2 * GRP * G
N1 = FF + FR
W2_AT = N1
W2T_AT = W2_AT + FT * C
NM = W2T_AT + C
NMD = N1 + C
NL = 3 * C + C
GATE_AT = NL
NLG = NL + EXPERTS
S = 64
NSKEW = S * (S - 1) // 2
VP = 126
VT = NSKEW // VP
TAYLOR = 12
SQUARINGS = 16


MLPS = EXPERTS * B + (LAYERS - 1) * B
ITEMS = MLPS + LAYERS


def mlps_of(block):
    layer, b = divmod(block, B)
    return range(EXPERTS * b, EXPERTS * b + EXPERTS) if layer == 0 else [EXPERTS * B + block - B]


def mlp_item(m):
    return 1 + m if m < 2 else m + 2 if m <= EXPERTS * B else m + 3


LAYER_ITEM = [0, 3, EXPERTS * B + 3]


def stages(block):
    out = []
    if block == 0:
        out += [("prep", 1), ("norm", 1, "msa"), ("qkv", 1), ("prep", 2), ("mods", 1, 0), ("prep", 3)]
    if block >= 1:
        out += after_attention(block - 1)
    if block == 1:
        out += [("mods", 1, 1)]
    if block == 2:
        out += [("mods", 2, 0), ("prep", LAYER_ITEM[2])]
    if block == 3:
        out += [("mods", 2, 1)]
    if 1 <= block < BLOCKS - 1:
        out += [("norm", block + 1, "msa"), ("qkv", block + 1)]
    if block == BLOCKS - 1:
        out += [("norm", block - 1, "x"), ("rotate", 0)]
    return out


def after_attention(block):
    out = [("norm", block, "o"), ("proj", block), ("norm", block, "mlp")]
    if block // B == 0:
        out.append(("gate", block))
    for m in mlps_of(block):
        out.append(("mlp", m, block))
    if block // B == 0:
        out.append(("moe", block))
    return out


HEAD = [("mods", 0, 0), ("mods", 0, 1), ("prep", 0), ("norm", 0, "msa"), ("qkv", 0)]
TAIL = after_attention(BLOCKS - 1) + [("norm", BLOCKS - 1, "x"), ("rotate", 1)]

BANKS_OF = {"prep": (0, 0, 0), "mods": (1, 1), "norm": (2, 0, 0, 0, 0), "qkv": (1, 1, 2, 1, 2, 1, 2, 2),
            "proj": (1, 1), "gate": (1, 0), "mlp": (2, 2, 1, 1, 1), "moe": (0,), "rotate": (1, 1)}
PIECES = {"prep": 3, "mods": 2, "norm": 5, "qkv": 8, "proj": 2, "gate": 2, "mlp": 5, "moe": 1, "rotate": 2}


def due(block, unit):
    total = sum(PIECES[s[0]] for s in stages(block))
    first, last = (0 if block == 0 else 4), (UNITS if block == BLOCKS - 1 else UNITS - 8)
    upto = lambda u: total * max(0, min(u - first, last - first)) // (last - first)
    return upto(unit + 1) - upto(unit)


def solver_steps():
    out = [("v", t) for t in range(VT)] + [("v_rows",), ("p_load",)]
    out += [("mgs", j) for j in range(S)] + [("unit_cols",)]
    out += [("lu", j) for j in range(S)] + [("signs",), ("skew",), ("scale",)]
    out += [("taylor", n) for n in range(TAYLOR - 1, 0, -1)] + [("turned",)]
    out += [("square", i) for i in range(SQUARINGS)] + [("y",), ("m", 0), ("m", 1)]
    return out


STEPS = solver_steps()


def solver_due(block, unit):
    n = block * UNITS + unit
    total = len(STEPS)
    span = (BLOCKS - 1) * UNITS
    upto = lambda u: min(total, total * u // span)
    return range(upto(n), upto(n + 1))


SOLVER_BANK = ("v_rows", "p_load", "mgs", "lu", "skew", "taylor", "turned", "square", "y", "m")

MAX_SHARE = [3, 3, 3, 3, 2, 2, 0, 0]


def max_tiles(unit):
    at = sum(MAX_SHARE[:unit % 8])
    return [divmod(i, GRP) for i in range(at, at + MAX_SHARE[unit % 8])]


class Banks:

    def __init__(self, banks, drained):
        self.banks, self.drained, self.n = banks, drained, 0

    def take(self):
        i, before = self.n % 2, self.n // 2
        self.n += 1
        return self.banks[i], self.drained[i], before


def idle(ring, stage):
    for n in BANKS_OF[stage]:
        for _ in range(n):
            ring.take()
        yield


class Tally:

    def __init__(self):
        self.n = {}

    def next(self, name):
        self.n[name] = self.n.get(name, 0) + 1
        return self.n[name]


def build(nc, a, out):
    with ExitStack() as ctx:
        def sb(name, shape, dt=F32):
            return ctx.enter_context(nc.sbuf_tensor(name, shape, dt))

        def bank(name):
            return ctx.enter_context(nc.psum_tensor(name, [P, 512], F32))

        def sem(name):
            return ctx.enter_context(nc.semaphore(name))

        x_tok = sb("x_tok", [P, B * T, C])
        mod = sb("mod", [P, B, 2, 6, C])
        stat = sb("stat", [P, T, 6])
        mean_var = sb("mean_var", [P, T, 2])
        rstd = sb("rstd", [P, T])
        nwt = sb("nwt", [P, 2, 32])
        xn = sb("xn", [P, 2, C])
        xm = sb("xm", [P, C])
        h_tok = sb("h_tok", [P, 2, P + DW])
        h_hi = sb("h_hi", [P, N], F32R)
        h_lo = sb("h_lo", [P, N], F32R)
        h_d = sb("h_d", [DW, N], F32R)
        ada_a = sb("ada_a", [P, 6 * C])
        ada_d = sb("ada_d", [CR + 1, 6 * C])
        c_a = sb("c_a", [P, B])
        c_d = sb("c_d", [CR, B])
        c_row = sb("c_row", [P, B, C])
        e_a = sb("e_a", [P, B])
        e_d = sb("e_d", [CR, B])
        c_wide_a = sb("c_wide_a", [P, B, P])
        c_wide_d = sb("c_wide_d", [CR + 1, B, P])
        raw_a = sb("raw_a", [P, NM])
        raw_d = sb("raw_d", [DW, NMD + EXPERTS])
        lay_hi = sb("lay_hi", [P, 2, NLG], F32R)
        lay_lo = sb("lay_lo", [P, 2, NLG], F32R)
        lay_d = sb("lay_d", [DW, 2, NLG], F32R)
        ff_hi = sb("ff_hi", [P, 2, NM], F32R)
        ff_lo = sb("ff_lo", [P, 2, NM], F32R)
        ff_d = sb("ff_d", [DW, 2, NMD], F32R)
        ones_r = sb("ones_r", [DW, P], F32R)
        qkv_tok = sb("qkv_tok", [P, 2, 3 * C])
        qk_gain = sb("qk_gain", [P, 2, HD])
        qk_sq = sb("qk_sq", [P, 2 * NH, HD])
        qk_mean = sb("qk_mean", [P, 2 * NH])
        qk_var = sb("qk_var", [P, 2 * NH])
        qk_rstd = sb("qk_rstd", [P, 2 * NH])
        qs_tok = sb("qs_tok", [P, NH, 32], F32R)
        ks_tok = sb("ks_tok", [P, NH, 32], F32R)
        q_t = sb("q_t", [P, 2, G, N], F32R)
        k_t = sb("k_t", [P, 2, G, N], F32R)
        v_aug = sb("v_aug", [P, 2, T, NH * VW + 32])
        row_max = sb("row_max", [P, 2, T, P])
        probs = sb("probs", [P, PROBS, N])
        o_t = sb("o_t", [P, N])
        o_rden = sb("o_rden", [P, T, GRP])
        o_tok = sb("o_tok", [P, 2, T, C])
        gated = sb("gated", [P, 2, C])
        logits = sb("logits", [P, T, EXPERTS])
        g_cmp = sb("g_cmp", [P, 2, T * EXPERTS, EXPERTS])
        g_rank = sb("g_rank", [P, T, EXPERTS])
        g_sum = sb("g_sum", [P, T])
        lower = sb("lower", [P, EXPERTS, EXPERTS])
        cw = sb("cw", [P, T, EXPERTS])
        moe = sb("moe", [P, T, C])
        e_row = moe[:, 0:B, :]
        y_out = moe[:, :, :].rearrange("p (n t) c -> p n t c", n=2)
        g_raw = sb("g_raw", [P, 2, N])
        g_hi = sb("g_hi", [P, FT + 1, N], F32R)
        g_lo = sb("g_lo", [P, FT, N], F32R)
        ident = sb("ident", [P, P])
        w_rows = sb("w_rows", [VP, 2, 4, C])
        v_scr = sb("v_scr", [VP, C])
        v_col = sb("v_col", [VP, B, VT])
        vb_row = sb("vb_row", [B * VT, VP])
        v_row = sb("v_row", [B * VT, VP])
        p_nat = sb("p_nat", [P, S])
        p_nat_d = sb("p_nat_d", [CR, S])
        q_rows = sb("q_rows", [S, C])
        lu = sb("lu", [S, S])
        bc_row = sb("bc_row", [S, C])
        bc_sq = sb("bc_sq", [S, C])
        bc_scr = sb("bc_scr", [S, C])
        s_small = sb("s_small", [S, 8])
        s_norm = sb("s_norm", [S, 4])
        s_sign = sb("s_sign", [S, S])
        neg_after = sb("neg_after", [S, S])
        u_d = sb("u_d", [S, DW])
        skew = sb("skew", [S, B, S])
        skew_b = sb("skew_b", [S, B, S])
        rs_norm = sb("rs_norm", [S, 2, B])
        pow2 = sb("pow2", [S, SQUARINGS])
        sq_on = sb("sq_on", [S, B, SQUARINGS])
        sq_off = sb("sq_off", [S, B, SQUARINGS])
        sq_tmp = sb("sq_tmp", [S, B, SQUARINGS])
        e_scale = sb("e_scale", [S, B])
        rot = sb("rot", [S, B, 2, S])
        rot_new = sb("rot_new", [S, B, 2, S])
        y_t = sb("y_t", [S, B, C])
        m_hi = sb("m_hi", [P, B, C], F32R)
        m_lo = sb("m_lo", [P, B, C], F32R)
        m_d = sb("m_d", [DW, B, C], F32R)

        v_scratch = nc.dram_tensor("v_scratch", [B * VT, VP], F32, kind="Internal").ap()

        s_banks = [bank(f"s_bank{i}") for i in range(3)]
        o_bank = bank("o_bank")
        m_banks = [bank(f"m_bank{i}") for i in range(2)]
        d_banks = [bank(f"d_bank{i}") for i in range(2)]

        m_drained = [sem(f"m_drained{i}") for i in range(2)]
        d_drained = [sem(f"d_drained{i}") for i in range(2)]
        x_in = [sem(f"x_in{i}") for i in range(B)]
        c_in = sem("c_in")
        gain_in = sem("gain_in")
        ada_in = sem("ada_in")
        item_in = sem("item_in")
        p_in = sem("p_in")
        w_in = [sem(f"w_in{i}") for i in range(2)]
        scratch_in = sem("scratch_in")
        skew_in = sem("skew_in")
        y_stored = [sem(f"y_stored{i}") for i in range(2)]
        names = ("zeroed ident_ready consts_ready weights_ready c_exp c_wide mods_part mods_full xn_ready "
                 "h_tok_ready h_turned h_hi_ready qkv_full qk_normed stack_ready stack_turned scores_full probs_ready "
                 "pv_done o_copied o_turned o_taken max_full max_turned max_placed proj_full "
                 "gate_full gate_shifted gate_exp up_full g_hi_ready g_lo_ready down_full y_ready "
                 "dve_done pool_done solver_full row_squared col_done v_summed "
                 "norm_in norm_out rot_ready").split()
        s = {n: sem(n) for n in names}

        def ring_m():
            return Banks(m_banks, m_drained)

        def ring_d():
            return Banks(d_banks, d_drained)

        def layer_dmas(l):
            names_ = [("L0_cond_w_qkv", "L0_cond_b_qkv", "L0_cond_w_proj", "L0_cond_b_proj"),
                      ("L1_cond_w_qkv", "L1_cond_b_qkv", "L1_cond_w_proj", "L1_cond_b_proj"),
                      ("L2_cond_W_qkv", "L2_cond_b_qkv", "L2_cond_W_proj", "L2_cond_b_proj")][l]
            main, d = raw_a[:, :], raw_d[:, :]
            out_ = []
            for w, b, at, n in ((names_[0], names_[1], 0, 3 * C), (names_[2], names_[3], 3 * C, C)):
                out_.append((main[:, at:at + n], a[w][0:P, :]))
                for r in (0, 32, 64):
                    out_.append((d[r:r + CR, at:at + n], a[w][P:C, :]))
                for r in (16, 80):
                    out_.append((d[r:r + 1, at:at + n], a[b].rearrange("(o n) -> o n", o=1)))
            if l == 0:
                out_.append((main[:, GATE_AT:NLG], a["L0_cond_w_gate"][0:P, :]))
                for r in (0, 32, 64):
                    out_.append((d[r:r + CR, NMD:NMD + EXPERTS], a["L0_cond_w_gate"][P:C, :]))
            return out_

        def mlp_dmas(m):
            if m < EXPERTS * B:
                e = m % EXPERTS
                w1, b1 = a["L0_cond_w1"][e], a["L0_cond_b1"][e]
                w2, b2 = a["L0_cond_w2"][e], a["L0_cond_b2"][e]
            elif m < EXPERTS * B + B:
                w1, b1, w2, b2 = (a[f"L1_cond_{n}"] for n in ("w1", "b1", "w2", "b2"))
            else:
                w1, b1, w2, b2 = (a[f"L2_cond_{n}"] for n in ("W_fc1", "b_fc1", "W_fc2", "b_fc2"))
            row = lambda v: v.rearrange("(o n) -> o n", o=1)
            main, d = raw_a[:, :], raw_d[:, :]
            out_ = []
            for at, lo, n in ((0, 0, FF), (FF, FT * P, FR)):
                out_.append((main[:, at:at + n], w1[0:P, lo:lo + n]))
                for r in (0, 32, 64):
                    out_.append((d[r:r + CR, at:at + n], w1[P:C, lo:lo + n]))
                for r in (16, 80):
                    out_.append((d[r:r + 1, at:at + n], row(b1)[:, lo:lo + n]))
            out_.append((main[:, W2_AT:W2T_AT].rearrange("p (f n) -> p f n", f=FT),
                         w2[0:FT * P, :].rearrange("(f p) n -> p f n", p=P)))
            for r in (0, FR):
                out_.append((main[r:r + FR, W2T_AT:NM], w2[FT * P:FF, :]))
            for r in (0, 64):
                out_.append((d[r:r + 1, N1:NMD], row(b2)))
            return out_

        mlp_at = {mlp_item(m): m for m in range(MLPS)}
        item_dmas, staged = [], []
        for i in range(ITEMS):
            item_dmas.append(layer_dmas(LAYER_ITEM.index(i)) if i in LAYER_ITEM else mlp_dmas(mlp_at[i]))
            staged.append(16 * sum(len(dmas) for dmas in item_dmas))

        block = ctx.enter_context(nc.Block())

        @block.sync
        def _(sp):
            def load_item(i):
                if i == 0:
                    sp.wait_ge(s["zeroed"], 1)
                else:
                    sp.wait_ge(s["weights_ready"], i)
                for dst, src in item_dmas[i]:
                    sp.dma_start(dst, src).then_inc(item_in, 16)

            def load_ada(l):
                if l:
                    sp.wait_ge(s["mods_part"], 4 * l)
                w, b = [("L0_cond_w_adaln", "L0_cond_b_adaln"), ("L1_cond_w_mod", "L1_cond_b_mod"),
                        ("L2_cond_W_ada", "L2_cond_b_ada")][l]
                sp.dma_start(ada_a[:, :], a[w][0:P, :]).then_inc(ada_in, 16)
                sp.dma_start(ada_d[0:CR, :], a[w][P:C, :]).then_inc(ada_in, 16)
                sp.dma_start(ada_d[CR:CR + 1, :], a[b].rearrange("(o n) -> o n", o=1)).then_inc(ada_in, 16)

            def load_w(i):
                if i >= 2:
                    sp.wait_ge(s["v_summed"], 4 * (i - 1))
                sp.dma_start(w_rows[:, i % 2, :, :],
                             a["L3_cond_W"].rearrange("(t p) c -> p t c", p=VP)[:, 4 * i:4 * i + 4, :])\
                    .then_inc(w_in[i % 2], 16)

            cond = a["cond_1152"]
            sp.dma_start(c_row[:, :, :], cond.rearrange("(o b) c -> o b c", o=1).to_broadcast([P, B, C]))\
                .then_inc(c_in, 16)
            sp.dma_start(c_a[:, :], cond[:, 0:P].rearrange("b c -> c b"), allow_slow_non_contiguous=True)\
                .then_inc(c_in, 16)
            sp.dma_start(c_d[:, :], cond[:, P:C].rearrange("b c -> c b"), allow_slow_non_contiguous=True)\
                .then_inc(c_in, 16)
            load_ada(0)
            for b in range(B):
                sp.dma_start(x_tok[:, b * T:(b + 1) * T, :], a["x"][b].rearrange("(t p) c -> p t c", p=P))\
                    .then_inc(x_in[b], 16)
            load_item(0)
            for i, g in enumerate(("L1_cond_g_q", "L1_cond_g_k")):
                sp.dma_start(qk_gain[:, i, :], a[g].rearrange("(o n) -> o n", o=1).to_broadcast([P, HD]))\
                    .then_inc(gain_in, 16)
            load_item(1)
            load_w(0)
            load_w(1)
            for b in range(B):
                sp.dma_start(vb_row[b * VT:(b + 1) * VT, :], a["L3_cond_b"].rearrange("(t p) -> t p", p=VP))\
                    .then_inc(p_in, 16)
            sp.dma_start(p_nat[:, :], a["L3_cond_P"][0:P, :]).then_inc(p_in, 16)
            sp.dma_start(p_nat_d[:, :], a["L3_cond_P"][P:C, :]).then_inc(p_in, 16)
            load_item(2)
            load_ada(1)
            load_w(2)
            load_w(3)
            load_item(3)
            sp.wait_ge(scratch_in, 16)
            sp.wait_ge(s["consts_ready"], 1)
            flat = v_scratch.rearrange("(b t) p -> b (t p)", b=B)
            off = 0
            for i in range(S - 1):
                n = S - 1 - i
                sp.dma_start(skew[i:i + 1, :, i + 1:S], flat[:, off:off + n].rearrange("(o b) n -> o b n", o=1),
                             allow_slow_non_contiguous=(n == 1)).then_inc(skew_in, 16)
                off += n
            for i in range(4, ITEMS):
                if i == mlp_item(EXPERTS + 2):
                    load_ada(2)
                load_item(i)
            for n in range(2 * B):
                b, pair = divmod(n, 2)
                sp.wait_ge(s["y_ready"], n + 1)
                sp.dma_start(out[b].rearrange("(t p) c -> p t c", p=P)[:, 2 * pair:2 * pair + 2, :],
                             y_out[:, n % 2, :, :]).then_inc(y_stored[n % 2], 16)
            for i in range(2):
                sp.wait_ge(y_stored[i], 32)

        @block.gpsimd
        def _(pool):
            ring, mring, seen = ring_d(), ring_m(), Tally()
            done = [0]

            def link(ins):
                done[0] += 1
                ins.then_inc(s["pool_done"], 1)
                pool.wait_ge(s["pool_done"], done[0])

            pool.memset(raw_d[:, :], 0.0).then_inc(s["zeroed"], 1)
            link(pool.memset(ident[:, :], 0.0))
            pool.affine_select(out=ident[:, :], in_=ident[:, :], compare_op=ALU.not_equal, fill=1.0, base=0,
                               pattern=[[-1, P]], channel_multiplier=1).then_inc(s["ident_ready"], 1)
            link(pool.memset(h_tok[:, :, :], 0.0))
            for at in (C, P + 64 + CR):
                link(pool.memset(h_tok[:, :, at:at + 1], 1.0))
            link(pool.memset(qs_tok[:, :, :].bitcast(F32), 0.0))
            link(pool.memset(ks_tok[:, :, :].bitcast(F32), 0.0))
            link(pool.memset(ks_tok[:, :, MAXROW:MAXROW + 1].bitcast(F32), 1.0))
            link(pool.memset(v_aug[:, :, :, :], 1.0))
            link(pool.memset(ones_r[:, :].bitcast(F32), 1.0))
            link(pool.memset(lower[:, :, :], 1.0))
            link(pool.affine_select(out=lower[:, :, :], in_=lower[:, :, :], compare_op=ALU.is_gt, fill=0.0, base=0,
                                    pattern=[[1, EXPERTS], [-1, EXPERTS]], channel_multiplier=0))
            link(pool.memset(neg_after[:, :], -1.0))
            link(pool.affine_select(out=neg_after[:, :], in_=neg_after[:, :], compare_op=ALU.is_gt, fill=0.0, base=0,
                                    pattern=[[-1, S]], channel_multiplier=1))
            link(pool.memset(row_max[:, :, :, :], 0.0))
            link(pool.memset(u_d[:, :], 0.0))
            for i in range(SQUARINGS):
                pool.memset(pow2[:, i:i + 1], float(2 ** i)).then_inc(s["pool_done"], 1)
            done[0] += SQUARINGS
            pool.memset(skew[:, :, :], 0.0).then_inc(s["consts_ready"], 1)

            def prep(i):
                if i in LAYER_ITEM:
                    l = LAYER_ITEM.index(i)
                    na = NLG if l == 0 else NL
                    hi, lo, d = lay_hi[:, l % 2, :], lay_lo[:, l % 2, :], lay_d[:, l % 2, :]
                    cuts = [(0, 0, NL)] + ([(NL, NMD, EXPERTS)] if l == 0 else [])
                    if l == 2:
                        pool.wait_ge(s["gate_full"], B)
                else:
                    m = mlp_at[i]
                    na, cuts = NM, [(0, 0, NMD)]
                    hi, lo, d = ff_hi[:, m % 2, :], ff_lo[:, m % 2, :], ff_d[:, m % 2, :]
                    if m >= 2:
                        pool.wait_ge(s["down_full"], 2 * (m - 1))
                pool.wait_ge(item_in, staged[i])
                link(pool.tensor_copy(hi[:, 0:na], raw_a[:, 0:na]))
                yield
                pool.tensor_tensor(lo[:, 0:na], raw_a[:, 0:na], hi[:, 0:na].bitcast(F32), ALU.subtract)\
                    .then_inc(s["pool_done"], 1)
                done[0] += 1
                yield
                for to, frm, n in cuts:
                    link(pool.tensor_copy(d[:, to:to + n], raw_d[:, frm:frm + n]))
                for c, (to, frm, n) in enumerate(cuts):
                    ins = pool.tensor_tensor(d[64:DW, to:to + n], raw_d[64:DW, frm:frm + n],
                                             d[64:DW, to:to + n].bitcast(F32), ALU.subtract)
                    if c < len(cuts) - 1:
                        link(ins)
                ins.then_inc(s["weights_ready"], 1)
                pool.wait_ge(s["weights_ready"], i + 1)
                yield

            def norm(blk, kind):
                b, l = blk % B, blk // B
                mv = mod[:, b, l % 2, :, :]
                first = 0 if kind == "msa" else 3
                ring.take(), ring.take()
                for t in range(T):
                    if kind != "o":
                        pool.wait_ge(s["xn_ready"], seen.next("xn_ready"))
                    elif kind == "o" and t == 0:
                        pool.wait_ge(s["o_taken"], G * (blk + 1))
                    if seen.n.get("h_tok", 0) >= 2:
                        pool.wait_ge(s["h_turned"], seen.n["h_tok"] - 1)
                    seen.next("h_tok")
                    i = t % 2
                    d2 = h_tok[:, i, P + 32:P + DW].rearrange("p (r w) -> p r w", r=2)[:, :, 0:CR]
                    if kind in ("msa", "mlp"):
                        link(pool.tensor_tensor(xm[:, :], xn[:, i, :], mv[:, first + 1, :], ALU.mult))
                        link(pool.tensor_tensor(h_tok[:, i, 0:C], xm[:, :], mv[:, first, :], ALU.add))
                        src = h_tok[:, i, P:C]
                    else:
                        src_tile = o_tok[:, blk % 2, t, :] if kind == "o" else xn[:, i, :]
                        link(pool.tensor_copy(h_tok[:, i, 0:C], src_tile))
                        src = src_tile[:, P:C]
                    pool.tensor_copy(d2, src.unsqueeze(1).to_broadcast([P, 2, CR]))\
                        .then_inc(s["h_tok_ready"], 1)
                    yield
                yield

            def qkv(blk):
                l, i2 = blk // B, blk % 2

                def split(t):
                    tile = qkv_tok[:, t % 2, :]
                    heads = lambda at: tile[:, at:at + C].rearrange("p (h d) -> p h d", d=HD)
                    if l == 1:
                        pool.wait_ge(s["qk_normed"], seen.next("qk_normed"))
                    else:
                        pool.wait_ge(*copied[t])
                    if seen.n.get("stack", 0):
                        pool.wait_ge(s["stack_turned"], 2 * seen.n["stack"])
                    seen.next("stack")
                    for to, at, places in ((qs_tok, 0, (0, 1)), (ks_tok, C, (0, 2))):
                        for pl in places:
                            ins = pool.tensor_copy(to[:, :, HD * pl:HD * pl + HD], heads(at))
                            link(ins)
                    pool.tensor_tensor(qs_tok[:, :, 2 * HD:3 * HD], heads(0), qs_tok[:, :, 0:HD].bitcast(F32),
                                       ALU.subtract).then_inc(s["pool_done"], 1)
                    pool.tensor_tensor(ks_tok[:, :, HD:2 * HD], heads(C), ks_tok[:, :, 0:HD].bitcast(F32),
                                       ALU.subtract).then_inc(s["pool_done"], 1)
                    done[0] += 2
                    pool.tensor_copy(v_aug[:, i2, t, 0:NH * VW].rearrange("p (h w) -> p h w", w=VW)[:, :, 0:HD],
                                     heads(2 * C)).then_inc(s["stack_ready"], 1)

                copied = {}
                for t in range(T + 1):
                    if t < T:
                        _, drained, before = ring.take()
                        copied[t] = (drained, before + 1)
                        yield
                    if t > 0:
                        split(t - 1)
                        ring.take(), ring.take()
                        yield

            def mlp(m, blk):
                for tiles in ((0, 1), (2, 3), (4,)):
                    for f in tiles:
                        _, drained, before = ring.take()
                        pool.wait_ge(drained, before + 1)
                        pool.tensor_copy(g_hi[:, f, :], g_raw[:, seen.n.get("g", 0) % 2, :])\
                            .then_inc(s["g_hi_ready"], 1)
                        seen.next("g")
                    yield
                split = prep(mlp_item(m + 1)) if 1 <= m < MLPS - 1 else iter(())
                for pair in range(2):
                    ring.take()
                    for _ in range(2):
                        next(split, None)
                    yield

            def solver(step):
                if step[0] in SOLVER_BANK:
                    mring.take()
                if step[0] == "scale":
                    pool.wait_ge(s["norm_in"], 1)
                    pool.partition_all_reduce(rs_norm[:, 1, :], rs_norm[:, 0, :], S, RMAX).then_inc(s["norm_out"], 1)

            walk = {"prep": prep, "norm": norm, "qkv": qkv, "mlp": mlp}

            def side(todo):
                for st in todo:
                    yield from walk[st[0]](*st[1:]) if st[0] in walk else idle(ring, st[0])

            for _ in side(HEAD):
                pass
            for blk in range(BLOCKS):
                woven = side(stages(blk))
                for u in range(UNITS):
                    for _ in range(due(blk, u)):
                        next(woven)
                    for n in solver_due(blk, u):
                        solver(STEPS[n])
            for _ in side(TAIL):
                pass

        @block.scalar
        def _(act):
            ring, mring, seen = ring_d(), ring_m(), Tally()

            act.wait_ge(c_in, 48)
            act.activation(e_a[:, :], c_a[:, :], ACT.Exp, scale=-1.0).then_inc(s["c_exp"], 1)
            act.activation(e_d[:, :], c_d[:, :], ACT.Exp, scale=-1.0).then_inc(s["c_exp"], 1)
            act.activation(e_row, c_row[:, :, :], ACT.Exp, scale=-1.0).then_inc(s["c_exp"], 1)

            def exps(unit):
                for n in (2 * unit, 2 * unit + 1):
                    if n >= PROBS and n % GRP == 0:
                        act.wait_ge(s["pv_done"], (n - PROBS) // GRP + 1)
                    act.wait_ge(s["scores_full"], n + 1)
                    act.activation(probs[:, n % PROBS, :], s_banks[n % 3][:, :], ACT.Exp, scale=HD ** -0.5)\
                        .then_inc(s["probs_ready"], 1)

            def norm(blk, kind):
                (a_bank, _, _), (d_bank, _, _) = ring.take(), ring.take()
                for t in range(T):
                    seen.next("h_turned")
                    yield
                act.wait_ge(s["h_turned"], seen.n["h_turned"])
                act.activation(h_hi[:, :], a_bank[:, :], ACT.Copy).then_inc(s["h_hi_ready"], 1)
                act.activation(h_d[:, :], d_bank[0:DW, :], ACT.Copy).then_inc(s["h_hi_ready"], 1)
                yield

            def qkv(blk):
                for t in range(T + 1):
                    if t < T:
                        bk, drained, _ = ring.take()
                        act.wait_ge(s["qkv_full"], seen.next("qkv_full"))
                        act.activation(qkv_tok[:, t % 2, :], bk[:, 0:3 * C], ACT.Copy).then_inc(drained, 1)
                        yield
                    if t > 0:
                        (bk, drained, _), _ = ring.take(), ring.take()
                        act.wait_ge(s["stack_turned"], seen.next("stack_turned"))
                        seen.next("stack_turned")
                        act.activation(q_t[:, blk % 2, :, (t - 1) * P:t * P],
                                       bk[:, :].rearrange("p (g n) -> p g n", g=G), ACT.Copy).then_inc(drained, 1)
                        yield

            def gate(blk):
                ring.take()
                act.wait_ge(s["gate_shifted"], seen.next("gate_shifted"))
                act.activation(cw[:, :, :], logits[:, :, :], ACT.Exp).then_inc(s["gate_exp"], 1)
                yield
                yield

            def mlp(m, blk):
                for tiles in ((0, 1), (2, 3), (4,)):
                    for f in tiles:
                        bk, drained, _ = ring.take()
                        n = seen.next("up_full")
                        act.wait_ge(s["up_full"], n)
                        if n > 2:
                            act.wait_ge(s["g_lo_ready"], n - 2)
                        act.activation(g_raw[:, (n - 1) % 2, :], bk[:, :], ACT.Gelu_apprx_tanh).then_inc(drained, 1)
                    yield
                for pair in range(2):
                    ring.take()
                    yield

            def solver(step):
                if step[0] in SOLVER_BANK:
                    bk, drained, before = mring.take()
                    full = seen.next("solver_full")
                if step[0] == "v_rows":
                    act.wait_ge(drained, before + 1)
                    act.dma_start(v_scratch, v_row[:, :]).then_inc(scratch_in, 16)
                elif step[0] == "p_load":
                    act.wait_ge(s["solver_full"], full)
                    act.activation(q_rows[:, :], bk[0:S, 0:C], ACT.Copy).then_inc(drained, 1)
                elif step[0] == "mgs":
                    act.wait_ge(s["solver_full"], full)
                    act.activation(bc_row[:, :], bk[0:S, 0:C], ACT.Copy).then_inc(drained, 1)
                    act.wait_ge(drained, before + 1)
                    act.activation(bc_sq[:, :], bc_row[:, :], ACT.Square, accum_out=s_norm[:, 0:1])\
                        .then_inc(s["row_squared"], 1)
                elif step[0] == "lu":
                    act.wait_ge(s["solver_full"], full)
                    act.activation(bc_row[:, 0:S], bk[0:S, 0:S], ACT.Copy).then_inc(drained, 1)

            walk = {"norm": norm, "qkv": qkv, "gate": gate, "mlp": mlp}

            def side(todo):
                for st in todo:
                    yield from walk[st[0]](*st[1:]) if st[0] in walk else idle(ring, st[0])

            for _ in side(HEAD):
                pass
            for _ in range(T * GRP + 1):
                mring.take()
            for blk in range(BLOCKS):
                woven = side(stages(blk))
                for u in range(UNITS):
                    unit = blk * UNITS + u
                    exps(unit)
                    if unit // 8 + 1 < BLOCKS * G:
                        for _ in max_tiles(u):
                            mring.take()
                        if u % 8 == 6:
                            mring.take()
                    for _ in range(due(blk, u)):
                        next(woven)
                    for n in solver_due(blk, u):
                        solver(STEPS[n])
            for _ in side(TAIL):
                pass

        @block.vector
        def _(dve):
            ring, mring, seen = ring_d(), ring_m(), Tally()
            done = [0]

            def link(ins):
                done[0] += 1
                ins.then_inc(s["dve_done"], 1)
                dve.wait_ge(s["dve_done"], done[0])

            def rsqrt(y, v, t):
                link(dve.tensor_scalar(y.bitcast(I32), v.bitcast(I32), -0.5, 1597463007.0, ALU.mult, ALU.add))
                for _ in range(3):
                    link(dve.scalar_tensor_tensor(out=t, in0=v, scalar=-0.5, in1=y, op0=ALU.mult, op1=ALU.mult))
                    link(dve.tensor_tensor(t, t, y, ALU.mult))
                    link(dve.scalar_tensor_tensor(out=y, in0=t, scalar=1.5, in1=y, op0=ALU.add, op1=ALU.mult))

            link(dve.memset(c_wide_d[:, :, :], 1.0))
            dve.wait_ge(s["c_exp"], 3)
            for e, c in ((e_a[:, :], c_a[:, :]), (e_d[:, :], c_d[:, :]), (e_row, c_row[:, :, :])):
                link(dve.tensor_scalar(e, e, 1.0, None, ALU.add))
                link(dve.reciprocal(e, e))
                link(dve.tensor_tensor(c, c, e, ALU.mult))
                if c.shape[0] == P and len(c.shape) == 2:
                    dve.tensor_copy(c_wide_a[:, :, :], c_a[:, :].unsqueeze(2).to_broadcast([P, B, P]))\
                        .then_inc(s["c_wide"], 1)
                if c.shape[0] == CR:
                    dve.tensor_copy(c_wide_d[0:CR, :, :], c_d[:, :].unsqueeze(2).to_broadcast([CR, B, P]))\
                        .then_inc(s["c_wide"], 1)

            def take_max(grp, t, j):
                bk, drained, _ = mring.take()
                dve.wait_ge(s["max_full"], seen.next("max_full"))
                dve.tensor_reduce(row_max[:, grp % 2, t, MAXROW + 32 * j:MAXROW + 32 * j + 1], bk[:, :], AX.X, ALU.max).then_inc(drained, 1)

            def place_max(grp):
                bk, drained, before = mring.take()
                q = q_t[:, grp // G % 2, grp % G, :]
                dve.wait_ge(s["max_turned"], grp + 1)
                dve.scalar_tensor_tensor(out=q, in0=bk[:, :], scalar=-1.0, in1=q.bitcast(F32), op0=ALU.mult,
                                         op1=ALU.add).then_inc(drained, 1)
                dve.wait_ge(drained, before + 1)

            def o_copy(grp):
                dve.wait_ge(s["pv_done"], T * (grp + 1))
                dve.tensor_copy(o_t[:, :], o_bank[:, :]).then_inc(s["o_copied"], 1)

            def o_normalise(grp):
                dve.wait_ge(s["o_turned"], grp + 1)
                view = o_bank[:, :].rearrange("p (t j w) -> p t j w", t=T, j=GRP)
                link(dve.reciprocal(o_rden[:, :, :], view[:, :, :, HD]))
                g = grp % G
                dst = o_tok[:, grp // G % 2, :, g * GRP * HD:(g + 1) * GRP * HD].rearrange("p t (j d) -> p t j d", d=HD)
                dve.tensor_tensor(dst, view[:, :, :, 0:HD], o_rden[:, :, :].unsqueeze(3).to_broadcast([P, T, GRP, HD]),
                                  ALU.mult).then_inc(s["o_taken"], 1)

            def mods(l, b):
                for half in range(2):
                    bk, drained, before = ring.take()
                    dve.wait_ge(s["mods_full"], seen.next("mods_full"))
                    src = bk[:, 0:3 * C].rearrange("p (v c) -> p v c", v=3)
                    dst = mod[:, b, l % 2, 3 * half:3 * half + 3, :]
                    dve.tensor_copy(dst[:, 0:3:2, :], src[:, 0:3:2, :]).then_inc(s["mods_part"], 1)
                    dve.tensor_scalar(dst[:, 1, :], src[:, 1, :], 1.0, None, ALU.add).then_inc(drained, 1)
                    dve.wait_ge(drained, before + 1)
                    dve.wait_ge(s["mods_part"], seen.next("mods_part"))
                    yield

            def norm(blk, kind):
                b = blk % B
                (a_bank, a_free, _), (d_bank, d_free, _) = ring.take(), ring.take()
                for t in range(T):
                    tile = x_tok[:, b * T + t, :]
                    if kind == "msa" and blk < B and t == 0:
                        dve.wait_ge(x_in[b], 16)
                    if kind in ("msa", "mlp") and t == 0:
                        for i in range(T):
                            dve.bn_stats(stat[:, i, :], x_tok[:, b * T + i, :]).then_inc(s["dve_done"], 1)
                        done[0] += T
                        dve.wait_ge(s["dve_done"], done[0])
                        for i in range(T):
                            dve.bn_aggr(mean_var[:, i, :], stat[:, i, :]).then_inc(s["dve_done"], 1)
                        done[0] += T
                        dve.wait_ge(s["dve_done"], done[0])
                        link(dve.tensor_scalar(nwt[:, 1, 0:T], mean_var[:, :, 1], EPS, None, ALU.add))
                        rsqrt(rstd[:, :], nwt[:, 1, 0:T], nwt[:, 0, 0:T])
                    if kind != "o":
                        n = seen.next("xn")
                        if n > 2:
                            dve.wait_ge(s["h_tok_ready"], xn_use[-2])
                        if kind == "x":
                            dve.tensor_copy(xn[:, (n - 1) % 2, :], tile).then_inc(s["xn_ready"], 1)
                        else:
                            dve.tensor_scalar(xn[:, (n - 1) % 2, :], tile, mean_var[:, t, 0:1], rstd[:, t:t + 1],
                                              ALU.subtract, ALU.mult).then_inc(s["xn_ready"], 1)
                    h_uses[0] += 1
                    if kind != "o":
                        xn_use.append(h_uses[0])
                    yield
                dve.wait_ge(s["h_hi_ready"], 2 * (h_uses[0] // T))
                dve.tensor_tensor(h_lo[:, :], a_bank[:, :], h_hi[:, :].bitcast(F32), ALU.subtract)\
                    .then_inc(a_free, 1)
                dve.tensor_tensor(h_d[32:64, :], d_bank[32:64, :], h_d[32:64, :].bitcast(F32), ALU.subtract)\
                    .then_inc(d_free, 1)
                yield

            h_uses, xn_use = [0], []

            def qkv(blk):
                l = blk // B
                for t in range(T + 1):
                    if t < T:
                        _, drained, before = ring.take()
                        if l == 1:
                            if blk == B and t == 0:
                                dve.wait_ge(gain_in, 32)
                            dve.wait_ge(drained, before + 1)
                            qk = qkv_tok[:, t % 2, 0:2 * C].rearrange("p (h d) -> p h d", d=HD)
                            wide = lambda v: v.unsqueeze(2).to_broadcast([P, 2 * NH, HD])
                            link(dve.tensor_reduce(qk_mean[:, :], qk, AX.X, ALU.add))
                            link(dve.tensor_scalar(qk_mean[:, :], qk_mean[:, :], 1.0 / HD, None, ALU.mult))
                            link(dve.tensor_tensor(qk, qk, wide(qk_mean[:, :]), ALU.subtract))
                            link(dve.tensor_tensor(qk_sq[:, :, :], qk, qk, ALU.mult))
                            link(dve.tensor_reduce(qk_var[:, :], qk_sq[:, :, :], AX.X, ALU.add))
                            link(dve.tensor_scalar(qk_var[:, :], qk_var[:, :], 1.0 / HD, EPS, ALU.mult, ALU.add))
                            rsqrt(qk_rstd[:, :], qk_var[:, :], nwt[:, 0, :])
                            link(dve.tensor_tensor(qk, qk, wide(qk_rstd[:, :]), ALU.mult))
                            g4 = qkv_tok[:, t % 2, 0:2 * C].rearrange("p (w h d) -> p w h d", w=2, d=HD)
                            dve.tensor_tensor(g4, g4, qk_gain[:, :, :].unsqueeze(2).to_broadcast([P, 2, NH, HD]),
                                              ALU.mult).then_inc(s["qk_normed"], 1)
                        yield
                    if t > 0:
                        _, (bk, drained, _) = ring.take(), ring.take()
                        seen.next("stack_turned")
                        dve.wait_ge(s["stack_turned"], seen.next("stack_turned"))
                        dve.tensor_copy(k_t[:, blk % 2, :, (t - 1) * P:t * P],
                                        bk[:, :].rearrange("p (g n) -> p g n", g=G)).then_inc(drained, 1)
                        yield

            def residual(bk, drained, before, blk, t0, vector):
                b, l = blk % B, blk // B
                gv = mod[:, b, l % 2, vector, :].unsqueeze(1).to_broadcast([P, 2, C])
                dve.tensor_tensor(gated[:, :, :], bk[:, 0:2 * C].rearrange("p (t c) -> p t c", t=2), gv, ALU.mult)\
                    .then_inc(drained, 1)
                dve.wait_ge(drained, before + 1)
                xs = x_tok[:, b * T + t0:b * T + t0 + 2, :]
                link(dve.tensor_tensor(xs, xs, gated[:, :, :], ALU.add))

            def proj(blk):
                for pair in range(2):
                    bk, drained, before = ring.take()
                    dve.wait_ge(s["proj_full"], seen.next("proj_full"))
                    residual(bk, drained, before, blk, 2 * pair, 2)
                    yield

            def gate(blk):
                bk, drained, before = ring.take()
                dve.wait_ge(s["gate_full"], seen.next("gate_full"))
                dve.tensor_copy(logits[:, :, :], bk[:, 0:T * EXPERTS].rearrange("p (t e) -> p t e", t=T))\
                    .then_inc(drained, 1)
                dve.wait_ge(drained, before + 1)
                e4 = [P, T, EXPERTS, EXPERTS]
                for i, op in ((0, ALU.is_gt), (1, ALU.is_equal)):
                    for t in range(T):
                        link(dve.tensor_tensor(g_cmp[:, i, EXPERTS * t:EXPERTS * t + EXPERTS, :],
                                               logits[:, t, :].unsqueeze(1).to_broadcast([P, EXPERTS, EXPERTS]),
                                               logits[:, t, :].unsqueeze(2).to_broadcast([P, EXPERTS, EXPERTS]), op))
                eq = g_cmp[:, 1, :, :].rearrange("p (t e) j -> p t e j", t=T)
                link(dve.tensor_tensor(eq, eq, lower[:, :, :].unsqueeze(1).to_broadcast(e4), ALU.mult))
                link(dve.tensor_tensor(g_cmp[:, 0, :, :], g_cmp[:, 0, :, :], g_cmp[:, 1, :, :], ALU.add))
                link(dve.tensor_reduce(g_rank[:, :, :].rearrange("p t e -> p (t e)"), g_cmp[:, 0, :, :], AX.X, ALU.add))
                link(dve.tensor_scalar(g_rank[:, :, :], g_rank[:, :, :], TOP_K - 0.5, None, ALU.is_lt))
                link(dve.tensor_reduce(g_sum[:, :], logits[:, :, :], AX.X, ALU.max))
                dve.tensor_tensor(logits[:, :, :], logits[:, :, :],
                                  g_sum[:, :].unsqueeze(2).to_broadcast([P, T, EXPERTS]), ALU.subtract)\
                    .then_inc(s["gate_shifted"], 1)
                yield
                dve.wait_ge(s["gate_exp"], seen.next("gate_exp"))
                link(dve.tensor_tensor(cw[:, :, :], cw[:, :, :], g_rank[:, :, :], ALU.mult))
                link(dve.tensor_reduce(g_sum[:, :], cw[:, :, :], AX.X, ALU.add))
                link(dve.reciprocal(g_sum[:, :], g_sum[:, :]))
                link(dve.tensor_tensor(cw[:, :, :], cw[:, :, :],
                                       g_sum[:, :].unsqueeze(2).to_broadcast([P, T, EXPERTS]), ALU.mult))
                yield

            def mlp(m, blk):
                for tiles in ((0, 1), (2, 3), (4,)):
                    for f in tiles:
                        ring.take()
                        n = seen.next("g_hi_ready")
                        dve.wait_ge(s["g_hi_ready"], n)
                        if f < FT:
                            dve.tensor_tensor(g_lo[:, f, :], g_raw[:, (n - 1) % 2, :], g_hi[:, f, :].bitcast(F32),
                                              ALU.subtract).then_inc(s["g_lo_ready"], 1)
                        else:
                            dve.tensor_tensor(g_hi[FR:P, f, :], g_raw[FR:P, (n - 1) % 2, :],
                                              g_hi[FR:P, f, :].bitcast(F32), ALU.subtract)\
                                .then_inc(s["g_lo_ready"], 1)
                    yield
                for pair in range(2):
                    bk, drained, before = ring.take()
                    dve.wait_ge(s["down_full"], seen.next("down_full"))
                    if blk // B == 0:
                        e = m % EXPERTS
                        for i in range(2):
                            t = 2 * pair + i
                            src, w = bk[:, i * C:(i + 1) * C], cw[:, t, e:e + 1]
                            if e == 0:
                                ins = dve.tensor_scalar(moe[:, t, :], src, w, None, ALU.mult)
                            else:
                                ins = dve.scalar_tensor_tensor(out=moe[:, t, :], in0=src, scalar=w,
                                                               in1=moe[:, t, :], op0=ALU.mult, op1=ALU.add)
                            if i == 0:
                                link(ins)
                        ins.then_inc(drained, 1)
                        dve.wait_ge(drained, before + 1)
                    else:
                        residual(bk, drained, before, blk, 2 * pair, 5)
                    yield

            def moe_out(blk):
                b, l = blk % B, blk // B
                gv = mod[:, b, l % 2, 5, :].unsqueeze(1).to_broadcast([P, T, C])
                link(dve.tensor_tensor(moe[:, :, :], moe[:, :, :], gv, ALU.mult))
                xs = x_tok[:, b * T:(b + 1) * T, :]
                link(dve.tensor_tensor(xs, xs, moe[:, :, :], ALU.add))
                yield

            def rotate(b):
                for pair in range(2):
                    n = 2 * b + pair
                    bk, drained, before = ring.take()
                    dve.wait_ge(s["proj_full"], seen.next("proj_full"))
                    dve.tensor_copy(gated[:, :, :], bk[:, 0:2 * C].rearrange("p (t c) -> p t c", t=2))\
                        .then_inc(drained, 1)
                    dve.wait_ge(drained, before + 1)
                    if n >= 2:
                        dve.wait_ge(y_stored[n % 2], 16)
                    t0 = b * T + 2 * pair
                    dve.tensor_tensor(y_out[:, n % 2, :, :], gated[:, :, :], x_tok[:, t0:t0 + 2, :], ALU.add)\
                        .then_inc(s["y_ready"], 1)
                    dve.wait_ge(s["y_ready"], n + 1)
                    yield

            eye = ident[0:S, 0:S]
            eyes = eye.unsqueeze(1).to_broadcast([S, B, S])

            def solver(step):
                kind = step[0]
                if kind in SOLVER_BANK:
                    bk, drained, before = mring.take()
                    full = seen.next("solver_full")

                def drain(ins):
                    ins.then_inc(drained, 1)
                    dve.wait_ge(drained, before + 1)

                if kind == "v":
                    t = step[1]
                    i = t // 4
                    dve.wait_ge(w_in[i % 2], 16 * (i // 2 + 1))
                    for b in range(B):
                        ins = dve.tensor_tensor_reduce(out=v_scr[:, :], in0=w_rows[:, i % 2, t % 4, :],
                                                       in1=c_row[0:VP, b, :], scale=1.0, scalar=0.0, op0=ALU.mult,
                                                       op1=ALU.add, accum_out=v_col[:, b, t:t + 1])
                        if b == 0:
                            link(ins)
                    ins.then_inc(s["v_summed"], 1)
                    dve.wait_ge(s["v_summed"], t + 1)
                elif kind == "v_rows":
                    dve.wait_ge(s["solver_full"], full)
                    dve.wait_ge(p_in, 64)
                    dve.tensor_tensor(v_row[:, :], bk[0:B * VT, 0:VP], vb_row[:, :], ALU.add).then_inc(drained, 1)
                elif kind == "mgs":
                    j = step[1]
                    dve.wait_ge(drained, before + 1)
                    link(dve.tensor_tensor_reduce(out=bc_scr[:, :], in0=q_rows[:, :], in1=bc_row[:, :], scale=1.0,
                                                  scalar=0.0, op0=ALU.mult, op1=ALU.add,
                                                  accum_out=s_small[:, 0:1]))
                    dve.wait_ge(s["row_squared"], j + 1)
                    link(dve.reciprocal(s_small[:, 1:2], s_norm[:, 0:1]))
                    link(dve.tensor_scalar(s_small[:, 2:3], s_small[:, 0:1], s_small[:, 1:2], neg_after[:, j:j + 1],
                                           ALU.mult, ALU.mult))
                    dve.scalar_tensor_tensor(out=q_rows[:, :], in0=bc_row[:, :], scalar=s_small[:, 2:3],
                                             in1=q_rows[:, :], op0=ALU.mult, op1=ALU.add)\
                        .then_inc(s["col_done"], 1)
                elif kind == "unit_cols":
                    dve.wait_ge(s["col_done"], S)
                    link(dve.tensor_tensor_reduce(out=bc_scr[:, :], in0=q_rows[:, :], in1=q_rows[:, :], scale=1.0,
                                                  scalar=0.0, op0=ALU.mult, op1=ALU.add,
                                                  accum_out=s_small[:, 0:1]))
                    rsqrt(s_small[:, 1:2], s_small[:, 0:1], s_small[:, 2:3])
                    link(dve.tensor_scalar(q_rows[:, :], q_rows[:, :], s_small[:, 1:2], None, ALU.mult))
                    dve.tensor_copy(lu[:, :], q_rows[:, 0:S]).then_inc(s["col_done"], 1)
                elif kind == "lu":
                    j = step[1]
                    dve.wait_ge(drained, before + 1)
                    w = bc_row[:, j:j + 1]
                    link(dve.tensor_scalar(s_sign[:, j:j + 1], w, 0.0, 2.0, ALU.is_ge, ALU.mult))
                    link(dve.scalar_tensor_tensor(out=s_small[:, 0:1], in0=s_sign[:, j:j + 1], scalar=-1.0, in1=w,
                                                  op0=ALU.add, op1=ALU.add))
                    link(dve.reciprocal(s_small[:, 1:2], s_small[:, 0:1]))
                    link(dve.tensor_scalar(s_small[:, 2:3], lu[:, j:j + 1], s_small[:, 1:2], neg_after[:, j:j + 1],
                                           ALU.mult, ALU.mult))
                    dve.scalar_tensor_tensor(out=lu[:, :], in0=bc_row[:, 0:S], scalar=s_small[:, 2:3],
                                             in1=lu[:, :], op0=ALU.mult, op1=ALU.add).then_inc(s["col_done"], 1)
                elif kind == "signs":
                    dve.wait_ge(s["col_done"], 1 + 2 * S)
                    link(dve.tensor_tensor_reduce(out=bc_scr[:, 0:S], in0=s_sign[:, :], in1=eye, scale=1.0,
                                                  scalar=0.0, op0=ALU.mult, op1=ALU.add,
                                                  accum_out=s_small[:, 0:1]))
                    link(dve.tensor_scalar(s_small[:, 1:2], s_small[:, 0:1], -1.0, 1.0, ALU.mult, ALU.add))
                    link(dve.tensor_scalar(q_rows[:, :], q_rows[:, :], s_small[:, 1:2], None, ALU.mult))
                    link(dve.tensor_copy(u_d[:, :].rearrange("p (r w) -> p r w", r=3)[:, :, 0:CR],
                                         q_rows[:, P:C].unsqueeze(1).to_broadcast([S, 3, CR])))
                elif kind == "skew":
                    dve.wait_ge(s["solver_full"], full)
                    drain(dve.tensor_tensor(skew_b[:, :, :], skew[:, :, :],
                                            bk[0:S, 0:B * S].rearrange("p (b n) -> p b n", b=B), ALU.subtract))
                    link(dve.scalar_tensor_tensor(out=rot_new[:, :, 0, :], in0=skew_b[:, :, :], scalar=-1.0,
                                                  in1=skew_b[:, :, :], op0=ALU.mult, op1=ALU.max))
                    dve.tensor_reduce(rs_norm[:, 0, :], rot_new[:, :, 0, :], AX.X, ALU.add)\
                        .then_inc(s["norm_in"], 1)
                elif kind == "scale":
                    dve.wait_ge(s["norm_out"], 1)
                    wide = [S, B, SQUARINGS]
                    powers = pow2[:, :].unsqueeze(1).to_broadcast(wide)
                    link(dve.tensor_tensor(sq_on[:, :, :], rs_norm[:, 1, :].unsqueeze(2).to_broadcast(wide), powers,
                                           ALU.is_gt))
                    link(dve.tensor_scalar(sq_off[:, :, :], sq_on[:, :, :], -1.0, 1.0, ALU.mult, ALU.add))
                    link(dve.tensor_tensor(sq_tmp[:, :, :], sq_on[:, :, :], powers, ALU.mult))
                    link(dve.tensor_reduce(e_scale[:, :], sq_tmp[:, :, :], AX.X, ALU.add))
                    link(dve.tensor_scalar(e_scale[:, :], e_scale[:, :], 1.0, None, ALU.add))
                    link(dve.reciprocal(e_scale[:, :], e_scale[:, :]))
                    for b in range(B):
                        link(dve.tensor_scalar(skew_b[:, b, :], skew_b[:, b, :], e_scale[:, b:b + 1], -1.0,
                                               ALU.mult, ALU.mult))
                    dve.scalar_tensor_tensor(out=rot[:, :, 0, :], in0=skew_b[:, :, :], scalar=-1.0 / TAYLOR,
                                             in1=eyes, op0=ALU.mult, op1=ALU.add).then_inc(s["rot_ready"], 1)
                elif kind == "taylor":
                    dve.wait_ge(s["solver_full"], full)
                    drain(dve.scalar_tensor_tensor(out=rot[:, :, 0, :],
                                                   in0=bk[0:S, 0:B * S].rearrange("p (b n) -> p b n", b=B),
                                                   scalar=1.0 / step[1], in1=eyes, op0=ALU.mult, op1=ALU.add))
                elif kind == "turned":
                    dve.wait_ge(s["solver_full"], full)
                    drain(dve.tensor_copy(rot[:, :, 1, :], bk[0:S, 0:B * S].rearrange("p (b n) -> p b n", b=B)))
                elif kind == "square":
                    i = step[1]
                    dve.wait_ge(s["solver_full"], full)
                    flat = lambda v: v.rearrange("p b r n -> p b (r n)")
                    on, off = (v[:, :, i:i + 1].to_broadcast([S, B, 2 * S]) for v in (sq_on, sq_off))
                    link(dve.tensor_tensor(flat(rot_new[:, :, :, :]),
                                           bk[0:S, 0:2 * B * S].rearrange("p (b n) -> p b n", b=B), on, ALU.mult))
                    link(dve.tensor_tensor(flat(rot[:, :, :, :]), flat(rot[:, :, :, :]), off, ALU.mult))
                    drain(dve.tensor_tensor(flat(rot[:, :, :, :]), flat(rot[:, :, :, :]),
                                            flat(rot_new[:, :, :, :]), ALU.add))
                elif kind == "y":
                    dve.tensor_tensor(rot[:, :, 1, :], rot[:, :, 1, :], eyes, ALU.subtract)\
                        .then_inc(s["rot_ready"], 1)
                    dve.wait_ge(s["solver_full"], full)
                    drain(dve.tensor_copy(y_t[:, :, :], bk[0:S, 0:B * C].rearrange("p (b n) -> p b n", b=B)))
                elif kind == "m":
                    b = step[1]
                    dve.wait_ge(s["solver_full"], full)
                    link(dve.tensor_copy(m_hi[:, b, :], bk[:, 0:C]))
                    link(dve.tensor_tensor(m_lo[:, b, :], bk[:, 0:C], m_hi[:, b, :].bitcast(F32), ALU.subtract))
                    link(dve.tensor_copy(m_d[:, b, :], bk[0:DW, 256:256 + C]))
                    drain(dve.tensor_tensor(m_d[64:DW, b, :], bk[64:DW, 256:256 + C],
                                            m_d[64:DW, b, :].bitcast(F32), ALU.subtract))

            walk = {"mods": mods, "norm": norm, "qkv": qkv, "proj": proj, "gate": gate, "mlp": mlp, "moe": moe_out,
                    "rotate": rotate}

            def side(todo):
                for st in todo:
                    yield from walk[st[0]](*st[1:]) if st[0] in walk else idle(ring, st[0])

            dve.wait_ge(s["consts_ready"], 1)
            for _ in side(HEAD):
                pass
            for t in range(T):
                for j in range(GRP):
                    take_max(0, t, j)
            place_max(0)
            for blk in range(BLOCKS):
                woven = side(stages(blk))
                for u in range(UNITS):
                    grp = blk * G + u // 8
                    if u % 8 == 2 and grp > 0:
                        o_copy(grp - 1)
                    if u % 8 == 3 and grp > 0:
                        o_normalise(grp - 1)
                    if grp + 1 < BLOCKS * G:
                        for t, j in max_tiles(u):
                            take_max(grp + 1, t, j)
                        if u % 8 == 6:
                            place_max(grp + 1)
                    for _ in range(due(blk, u)):
                        next(woven)
                    for n in solver_due(blk, u):
                        solver(STEPS[n])
            o_copy(BLOCKS * G - 1)
            o_normalise(BLOCKS * G - 1)
            for _ in side(TAIL):
                pass

        @block.tensor
        def _(pe):
            ring, mring, seen = ring_d(), ring_m(), Tally()
            placed = {}
            stacks = {}
            h_ready = []

            def take(r):
                bk, drained, before = r.take()
                if before:
                    pe.wait_ge(drained, before)
                return bk, (drained, before + 1)

            def linear(dst, h, w_hi, w_lo, w_d):
                h1, h2, hd = h
                pe.matmul(dst, h1, w_hi, start=True, stop=False)
                pe.matmul(dst, h2, w_hi, start=False, stop=False)
                pe.matmul(dst, h1, w_lo, start=False, stop=False)
                return pe.matmul(dst, hd, w_d, start=False, stop=True)

            def h_tile(t):
                cols = slice(t * P, (t + 1) * P)
                return h_hi[:, cols], h_lo[:, cols], h_d[:, cols]

            def scores(unit):
                grp, kt = unit // 8, unit % 8 // 2
                par, g = grp // G % 2, grp % G
                if unit % 8 == 0:
                    pe.wait_ge(*placed[grp])
                for i in range(2):
                    n, j = 2 * unit + i, 2 * (unit % 2) + i
                    rows = slice(32 * j, 32 * j + 32)
                    if n >= 3:
                        pe.wait_ge(s["probs_ready"], n - 2)
                    pe.matmul(s_banks[n % 3][:, :], k_t[rows, par, g, kt * P:(kt + 1) * P], q_t[rows, par, g, :],
                              start=True, stop=True).then_inc(s["scores_full"], 1)

            def max_scores(grp, t, j):
                par, g = grp // G % 2, grp % G
                rows = slice(32 * j, 32 * j + 32)
                if grp % G == 0 and t == 0 and j == 0:
                    for w in stacks[grp // G]:
                        pe.wait_ge(*w)
                bk, _ = take(mring)
                pe.matmul(bk[:, :], q_t[rows, par, g, t * P:(t + 1) * P], k_t[rows, par, g, :],
                          start=True, stop=True).then_inc(s["max_full"], 1)

            def max_turn(grp):
                for i in range(2):
                    pe.wait_ge(m_drained[i], (mring.n + 1 - i) // 2)
                bk, placed[grp] = take(mring)
                for t in range(T):
                    ins = pe.transpose(bk[:, t * P:(t + 1) * P], row_max[:, grp % 2, t, :], ident[:, :])
                ins.then_inc(s["max_turned"], 1)

            def pv(quad):
                grp, kt = quad // T, quad % T
                par, g = grp // G % 2, grp % G
                pe.wait_ge(s["probs_ready"], GRP * (quad + 1))
                if kt == 0 and grp > 0:
                    pe.wait_ge(s["o_taken"], grp)
                for j in range(GRP):
                    at = (g * GRP + j) * VW
                    ins = pe.matmul(o_bank[32 * j:32 * j + 32, :], v_aug[:, par, kt, at:at + 32],
                                    probs[:, (GRP * quad + j) % PROBS, :],
                                    start=(kt == 0), stop=(kt == T - 1), skip_group_check=True)
                ins.then_inc(s["pv_done"], 1)

            def o_turn(grp):
                pe.wait_ge(s["o_copied"], grp + 1)
                for t in range(T):
                    ins = pe.transpose(o_bank[:, t * P:(t + 1) * P], o_t[:, t * P:(t + 1) * P], ident[:, :])
                ins.then_inc(s["o_turned"], 1)

            def mods(l, b):
                for half in range(2):
                    bk, _ = take(ring)
                    pe.wait_ge(ada_in, 48 * (l + 1))
                    pe.wait_ge(s["c_wide"], 2)
                    cols = slice(3 * C * half, 3 * C * (half + 1))
                    pe.matmul(bk[:, 0:3 * C], c_wide_a[:, b, :], ada_a[:, cols], start=True, stop=False)
                    pe.matmul(bk[:, 0:3 * C], c_wide_d[:, b, :], ada_d[:, cols], start=False, stop=True)\
                        .then_inc(s["mods_full"], 1)
                    yield

            def norm(blk, kind):
                (a_bank, a_done), (d_bank, d_done) = take(ring), take(ring)
                for t in range(T):
                    n = seen.next("h_tok_ready")
                    pe.wait_ge(s["h_tok_ready"], n)
                    cols, i = slice(t * P, (t + 1) * P), (n - 1) % 2
                    pe.transpose(a_bank[:, cols], h_tok[:, i, 0:P], ident[:, :])
                    pe.transpose(d_bank[0:DW, cols], h_tok[:, i, P:P + DW], ident[:, :]).then_inc(s["h_turned"], 1)
                    yield
                h_ready[:] = [a_done, d_done]
                yield

            def h_wait():
                for w in h_ready:
                    pe.wait_ge(*w)

            def qkv(blk):
                l = blk // B
                for t in range(T + 1):
                    if t < T:
                        bk, _ = take(ring)
                        if t == 0:
                            h_wait()
                            pe.wait_ge(s["weights_ready"], LAYER_ITEM[l] + 1)
                        linear(bk[:, 0:3 * C], h_tile(t), lay_hi[:, l % 2, 0:3 * C], lay_lo[:, l % 2, 0:3 * C],
                               lay_d[:, l % 2, 0:3 * C]).then_inc(s["qkv_full"], 1)
                        yield
                    if t > 0:
                        (qb, q_done), (kb, k_done) = take(ring), take(ring)
                        pe.wait_ge(s["stack_ready"], seen.next("stack_ready"))
                        for bk, src in ((qb, qs_tok), (kb, ks_tok)):
                            for g in range(G):
                                ins = pe.transpose(bk[:, g * P:(g + 1) * P],
                                                   src[:, g * GRP:(g + 1) * GRP, :].rearrange("p h w -> p (h w)")
                                                   .bitcast(F32), ident[:, :])
                            ins.then_inc(s["stack_turned"], 1)
                        stacks[blk] = [q_done, k_done] if t == 1 else stacks[blk] + [q_done, k_done]
                        yield

            def pair_linear(bk, pair, parts, signal):
                for i in range(2):
                    ins = linear(bk[:, i * C:(i + 1) * C], h_tile(2 * pair + i), *parts)
                ins.then_inc(signal, 1)

            def proj(blk):
                l = blk // B
                cols = slice(3 * C, 4 * C)
                for pair in range(2):
                    bk, _ = take(ring)
                    h_wait()
                    pair_linear(bk, pair, (lay_hi[:, l % 2, cols], lay_lo[:, l % 2, cols], lay_d[:, l % 2, cols]), s["proj_full"])
                    yield

            def gate(blk):
                bk, _ = take(ring)
                h_wait()
                cols = slice(GATE_AT, NLG)
                for t in range(T):
                    ins = linear(bk[:, t * EXPERTS:(t + 1) * EXPERTS], h_tile(t), lay_hi[:, 0, cols],
                                 lay_lo[:, 0, cols], lay_d[:, 0, cols])
                ins.then_inc(s["gate_full"], 1)
                yield
                yield

            def mlp(m, blk):
                i = m % 2
                for tiles in ((0, 1), (2, 3), (4,)):
                    for f in tiles:
                        bk, _ = take(ring)
                        if f == 0:
                            h_wait()
                            pe.wait_ge(s["weights_ready"], mlp_item(m) + 1)
                        c = slice(f * P, (f + 1) * P)
                        pe.matmul(bk[:, :], ff_hi[:, i, c], h_hi[:, :], start=True, stop=False)
                        pe.matmul(bk[:, :], ff_hi[:, i, c], h_lo[:, :], start=False, stop=False)
                        pe.matmul(bk[:, :], ff_lo[:, i, c], h_hi[:, :], start=False, stop=False)
                        pe.matmul(bk[:, :], ff_d[:, i, c], h_d[:, :], start=False, stop=True)\
                            .then_inc(s["up_full"], 1)
                    yield
                for pair in range(2):
                    bk, _ = take(ring)
                    pe.wait_ge(s["g_lo_ready"], (FT + 1) * (m + 1))
                    for k in range(2):
                        t = 2 * pair + k
                        dst, cols = bk[:, k * C:(k + 1) * C], slice(t * P, (t + 1) * P)
                        for f in range(FT):
                            w = slice(W2_AT + f * C, W2_AT + (f + 1) * C)
                            pe.matmul(dst, g_hi[:, f, cols], ff_hi[:, i, w], start=(f == 0), stop=False)
                            pe.matmul(dst, g_lo[:, f, cols], ff_hi[:, i, w], start=False, stop=False)
                            pe.matmul(dst, g_hi[:, f, cols], ff_lo[:, i, w], start=False, stop=False)
                        w = slice(W2T_AT, NM)
                        pe.matmul(dst, g_hi[:, FT, cols], ff_hi[:, i, w], start=False, stop=False)
                        pe.matmul(dst, g_hi[0:FR, FT, cols], ff_lo[0:FR, i, w], start=False, stop=False)
                        ins = pe.matmul(dst, ones_r[:, :], ff_d[:, i, N1:NMD], start=False, stop=True)
                    ins.then_inc(s["down_full"], 1)
                    yield

            def rotate(b):
                for pair in range(2):
                    bk, _ = take(ring)
                    h_wait()
                    pe.wait_ge(*m_ready[b])
                    pair_linear(bk, pair, (m_hi[:, b, :], m_lo[:, b, :], m_d[:, b, :]), s["proj_full"])
                    yield

            m_ready = {}
            last = [None]

            def solver(step):
                kind = step[0]
                if kind not in SOLVER_BANK:
                    return
                bk, ready = take(mring)
                if kind == "v_rows":
                    pe.wait_ge(s["v_summed"], VT)
                    ins = pe.transpose(bk[0:B * VT, 0:VP], v_col[:, :, :].rearrange("p b t -> p (b t)"),
                                       ident[0:VP, 0:VP])
                elif kind == "p_load":
                    pe.wait_ge(p_in, 64)
                    pe.transpose(bk[0:S, 0:P], p_nat[:, :], ident[:, :])
                    ins = pe.transpose(bk[0:S, P:C], p_nat_d[:, :], ident[0:CR, 0:CR])
                elif kind in ("mgs", "lu"):
                    j = step[1]
                    src = q_rows[:, :] if kind == "mgs" else lu[:, :]
                    if kind == "mgs" and j == 0:
                        pe.wait_ge(*last[0])
                    else:
                        pe.wait_ge(s["col_done"], j if kind == "mgs" else 1 + S + j)
                    ins = pe.matmul(bk[0:S, 0:src.shape[1]], ident[0:S, j:j + 1].to_broadcast([S, S]), src,
                                    start=True, stop=True)
                elif kind == "skew":
                    pe.wait_ge(skew_in, 16 * (S - 1))
                    for b in range(B):
                        ins = pe.transpose(bk[0:S, b * S:(b + 1) * S], skew[:, b, :], ident[0:S, 0:S])
                elif kind == "taylor":
                    if step[1] == TAYLOR - 1:
                        pe.wait_ge(s["rot_ready"], 1)
                    else:
                        pe.wait_ge(*last[0])
                    for b in range(B):
                        ins = pe.matmul(bk[0:S, b * S:(b + 1) * S], skew_b[:, b, :], rot[:, b, 0, :],
                                        start=True, stop=True)
                elif kind == "turned":
                    pe.wait_ge(*last[0])
                    for b in range(B):
                        ins = pe.transpose(bk[0:S, b * S:(b + 1) * S], rot[:, b, 0, :], ident[0:S, 0:S])
                elif kind == "square":
                    pe.wait_ge(*last[0])
                    for b in range(B):
                        for r in range(2):
                            at = (2 * b + r) * S
                            ins = pe.matmul(bk[0:S, at:at + S], rot[:, b, 1 - r, :], rot[:, b, r, :],
                                            start=True, stop=True)
                elif kind == "y":
                    pe.wait_ge(s["rot_ready"], 2)
                    for b in range(B):
                        ins = pe.matmul(bk[0:S, b * C:(b + 1) * C], rot[:, b, 1, :], q_rows[:, :],
                                        start=True, stop=True)
                elif kind == "m":
                    b = step[1]
                    if b == 0:
                        pe.wait_ge(*last[0])
                    pe.matmul(bk[:, 0:C], q_rows[:, 0:P], y_t[:, b, :], start=True, stop=True)
                    ins = pe.matmul(bk[0:DW, 256:256 + C], u_d[:, :], y_t[:, b, :], start=True, stop=True)
                    m_ready[b] = ready
                ins.then_inc(s["solver_full"], 1)
                last[0] = ready

            walk = {"mods": mods, "norm": norm, "qkv": qkv, "proj": proj, "gate": gate, "mlp": mlp,
                    "rotate": rotate}

            def side(todo):
                for st in todo:
                    yield from walk[st[0]](*st[1:]) if st[0] in walk else idle(ring, st[0])

            pe.wait_ge(s["ident_ready"], 1)
            pe.wait_ge(s["consts_ready"], 1)
            for _ in side(HEAD):
                pass
            for t in range(T):
                for j in range(GRP):
                    max_scores(0, t, j)
            max_turn(0)
            for blk in range(BLOCKS):
                woven = side(stages(blk))
                for u in range(UNITS):
                    unit = blk * UNITS + u
                    grp = unit // 8
                    scores(unit)
                    if u % 8 == 2 and grp > 0:
                        o_turn(grp - 1)
                    if grp + 1 < BLOCKS * G:
                        for t, j in max_tiles(u):
                            max_scores(grp + 1, t, j)
                        if u % 8 == 6:
                            max_turn(grp + 1)
                    if u % 2 == 1 and unit >= 3:
                        pv((unit - 3) // 2)
                    for _ in range(due(blk, u)):
                        next(woven)
                    for n in solver_due(blk, u):
                        solver(STEPS[n])
            pv(T * BLOCKS * G - 1)
            o_turn(BLOCKS * G - 1)
            for _ in side(TAIL):
                pass


def kernel(**inputs):
    import numpy as _np
    import concourse.bacc as _bacc
    from concourse.bass_utils import run_bass_kernel_spmd as _run

    nc = _bacc.Bacc("TRN2", target_bir_lowering=False, num_devices=1)
    arrays, args = {}, {}
    for name, value in inputs.items():
        v = _np.ascontiguousarray(value)
        arrays[f"in_{name}_dram"] = v
        args[name] = nc.dram_tensor(f"in_{name}_dram", v.shape, mybir.dt.from_np(v.dtype), kind="ExternalInput").ap()
    out = nc.dram_tensor("out_0_dram", (B, N, C), F32, kind="ExternalOutput").ap()
    build(nc, args, out)
    r = _run(nc, [arrays], core_ids=[0])
    return r.results[0]["out_0_dram"]
```

```python
from contextlib import ExitStack

import concourse.bass as bass
from concourse import mybir

F32 = mybir.dt.float32
F32R = mybir.dt.float32r
I32 = mybir.dt.int32
ALU = mybir.AluOpType
ACT = mybir.ActivationFunctionType
AX = mybir.AxisListType
RMAX = bass.bass_isa.ReduceOp.max

P = 128
B, N, C = 2, 512, 144
NH, HD = 16, 9
T = N // P
CR = C - P
LAYERS, EXPERTS, TOP_K = 3, 4, 2
FF = 4 * C
FT = FF // P
FR = FF - FT * P
DW = 96
EPS = 1e-6
GRP = 4
G = NH // GRP
S_BANKS, M_BANKS, D_BANKS = 2, 3, 2
PROBS = 8
MAXROW = 3 * HD
VW = HD + 1
BLOCKS = LAYERS * B
STEPS = T * NH
GSTEPS = T * GRP
N1 = FF + FR
W2_AT = N1
W2T_AT = W2_AT + FT * C
NM = W2T_AT + C
NMD = N1 + C
NL = 3 * C + C
GATE_AT = NL
NLG = NL + EXPERTS
S = 64
NSKEW = S * (S - 1) // 2
VP = 126
VT = NSKEW // VP
TAYLOR = 12
WCH = 2
SQUARINGS = 16


MLPS = EXPERTS * B + (LAYERS - 1) * B
ITEMS = MLPS + LAYERS


def mlps_of(block):
    layer, b = divmod(block, B)
    return range(EXPERTS * b, EXPERTS * b + EXPERTS) if layer == 0 else [EXPERTS * B + block - B]


def mlp_item(m):
    return 1 + m if m < 2 else m + 2 if m <= EXPERTS * B else m + 3


LAYER_ITEM = [0, 3, EXPERTS * B + 3]


def stages(block):
    out = []
    if block == 0:
        out += [("norm", 1, "msa"), ("qkv", 1), ("prep", 1), ("prep", 2), ("mods", 1, 0), ("prep", 3)]
    if block >= 1:
        out += after_attention(block - 1)
    if block == 1:
        out += [("mods", 1, 1)]
    if block == 2:
        out += [("mods", 2, 0), ("prep", LAYER_ITEM[2])]
    if block == 3:
        out += [("mods", 2, 1)]
    if 1 <= block < BLOCKS - 1:
        out += [("norm", block + 1, "msa"), ("qkv", block + 1)]
    if block == BLOCKS - 1:
        out += [("norm", block - 1, "x"), ("rotate", 0)]
    return out


def after_attention(block):
    out = [("norm", block, "o"), ("proj", block), ("norm", block, "mlp")]
    if block // B == 0:
        out.append(("gate", block))
    for m in mlps_of(block):
        out.append(("mlp", m, block))
    return out


HEAD = [("mods", 0, 0), ("mods", 0, 1), ("prep", 0), ("norm", 0, "msa"), ("qkv", 0)]
TAIL = after_attention(BLOCKS - 1) + [("norm", BLOCKS - 1, "x"), ("rotate", 1)]
WOVEN = [st for block in range(BLOCKS) for st in stages(block)]

BANKS_OF = {"prep": (), "mods": (2,), "norm": (0, 2, 0), "qkv": (2, 2, 2, 2, 2, 2), "proj": (2,), "gate": (1, 0),
            "mlp": (7, 0), "rotate": (2,)}


ROOM = {"prep": (), "mods": (1,), "norm": (4, 1, 2), "qkv": (2, 2, 2, 2, 2, 2), "proj": (2,), "gate": (2, 1),
        "mlp": (1, 1), "rotate": (1,)}


def slot_steps():
    steps = [0] * (BLOCKS * STEPS)
    for block in range(BLOCKS):
        first, last = (0 if block == 0 else 4), (STEPS if block == BLOCKS - 1 else STEPS - GSTEPS - 2)
        room = [w for st in stages(block) for w in ROOM[st[0]]]
        for i in range(len(room)):
            steps[block * STEPS + first + sum(room[:i]) * (last - first) // sum(room)] += 1
    return steps


SLOTS = slot_steps()


V_CHAIN = [("v", t) for t in range(VT)] + [("v_rows",)]
QR_CHAIN = [("p_load",)] + [("mgs", j) for j in range(S)] + [("unit_cols",)]
QR_CHAIN += [("lu", j) for j in range(S)] + [("signs",), ("less_one",), ("y",), ("m", 0), ("m", 1)]
EXP_CHAIN = [("skew",), ("scale",)] + [("taylor", n) for n in range(TAYLOR - 1, 0, -1)] + [("turned",)]
EXP_CHAIN += [("square", i) for i in range(SQUARINGS)]


HEAD_FROM = 3
HEAD_SLOTS = sum(len(BANKS_OF[st[0]]) for st in HEAD)
EARLY = HEAD_SLOTS - HEAD_FROM + T * GRP // 2
QR_PACE = 5
EXP_FROM = 141


def solver_plan():
    plan = [[] for _ in range(BLOCKS * STEPS)]
    for i, part in enumerate(V_CHAIN):
        plan[2 * i + 1].append(part)
    for i, part in enumerate(QR_CHAIN[EARLY:]):
        plan[i * QR_PACE // 2].append(part)
    for i, part in enumerate(EXP_CHAIN):
        plan[EXP_FROM + 4 * i].append(part)
    last = {part: n for n, parts in enumerate(plan) for part in parts}
    assert last[EXP_CHAIN[-1]] < last[("less_one",)] and last[QR_CHAIN[-1]] < BLOCKS * STEPS - GSTEPS
    return plan


SOLVER_PLAN = solver_plan()


def head_parts(slot):
    return QR_CHAIN[slot - HEAD_FROM:slot - HEAD_FROM + 1] if slot >= HEAD_FROM else []


def first_parts(i):
    at = HEAD_SLOTS - HEAD_FROM + i // 2
    return QR_CHAIN[at:at + 1] if i % 2 else []


SOLVER_BANK = ("v_rows", "p_load", "mgs", "lu", "skew", "taylor", "turned", "square", "y", "m")

MAX_SHARE = [2, 2] + [1] * (GSTEPS - 4) + [0, 0]
TURN_AT = GSTEPS - 2


def max_tiles(step):
    at = sum(MAX_SHARE[:step % GSTEPS])
    return [divmod(i, GRP) for i in range(at, at + MAX_SHARE[step % GSTEPS])]


class Banks:

    def __init__(self, banks, drained):
        self.banks, self.drained, self.n = banks, drained, 0

    def take(self):
        before, i = divmod(self.n, len(self.banks))
        self.n += 1
        return self.banks[i], self.drained[i], before


def idle(ring, stage):
    for n in BANKS_OF[stage]:
        for _ in range(n):
            ring.take()
        yield


class Tally:

    def __init__(self):
        self.n = {}

    def next(self, name):
        self.n[name] = self.n.get(name, 0) + 1
        return self.n[name]


def build(nc, a, out):
    with ExitStack() as ctx:
        def sb(name, shape, dt=F32):
            return ctx.enter_context(nc.sbuf_tensor(name, shape, dt))

        def bank(name):
            return ctx.enter_context(nc.psum_tensor(name, [P, 512], F32))

        def sem(name):
            return ctx.enter_context(nc.semaphore(name))

        x_tok = sb("x_tok", [P, B * T, C])
        mod = sb("mod", [P, B, 2, 6, C])
        stat = sb("stat", [P, T, 6])
        mean_var = sb("mean_var", [P, T, 2])
        rstd = sb("rstd", [P, T])
        nwt = sb("nwt", [P, 2, 32])
        h_tok = sb("h_tok", [P, T, P + DW])
        h_hi = sb("h_hi", [P, N], F32R)
        h_lo = sb("h_lo", [P, N], F32R)
        h_d = sb("h_d", [DW, N], F32R)
        ada_a = sb("ada_a", [P, 6 * C])
        ada_d = sb("ada_d", [CR + 1, 6 * C])
        c_a = sb("c_a", [P, B])
        c_d = sb("c_d", [CR, B])
        c_row = sb("c_row", [P, B, C])
        e_a = sb("e_a", [P, B])
        e_d = sb("e_d", [CR, B])
        c_wide_a = sb("c_wide_a", [P, B, P])
        c_wide_d = sb("c_wide_d", [CR + 1, B, P])
        raw_a = sb("raw_a", [P, NM])
        raw_d = sb("raw_d", [DW, NMD + EXPERTS])
        lay_hi = sb("lay_hi", [P, 2, NLG], F32R)
        lay_lo = sb("lay_lo", [P, 2, NLG], F32R)
        lay_d = sb("lay_d", [DW, 2, NLG], F32R)
        ff_hi = sb("ff_hi", [P, 2, NM], F32R)
        ff_lo = sb("ff_lo", [P, 2, NM], F32R)
        ff_d = sb("ff_d", [DW, 2, NMD], F32R)
        ones_r = sb("ones_r", [DW, P], F32R)
        qkv_tok = sb("qkv_tok", [P, T, 3 * C])
        qk_gain = sb("qk_gain", [P, 2, HD])
        qk_sq = sb("qk_sq", [P, 2 * NH, HD])
        qk_mean = sb("qk_mean", [P, 2 * NH])
        qk_var = sb("qk_var", [P, 2 * NH])
        qk_rstd = sb("qk_rstd", [P, 2 * NH])
        qs_tok = sb("qs_tok", [P, NH, 32], F32R)
        ks_tok = sb("ks_tok", [P, NH, 32], F32R)
        q_t = sb("q_t", [P, 2, G, N], F32R)
        k_t = sb("k_t", [P, 2, G, N], F32R)
        v_aug = sb("v_aug", [P, 2, T, NH * VW + 32])
        row_max = sb("row_max", [P, 2, T, P], F32R)
        probs = sb("probs", [P, PROBS, N])
        o_t = sb("o_t", [P, N])
        o_rden = sb("o_rden", [P, T, GRP])
        o_tok = sb("o_tok", [P, 2, T, C])
        gated = sb("gated", [P, 2, C])
        logits = sb("logits", [P, T, EXPERTS])
        g_cmp = sb("g_cmp", [P, 2, T * EXPERTS, EXPERTS])
        g_rank = sb("g_rank", [P, T, EXPERTS])
        g_sum = sb("g_sum", [P, T])
        lower = sb("lower", [P, EXPERTS, EXPERTS])
        cw = sb("cw", [P, T, EXPERTS])
        moe = sb("moe", [P, T, C])
        e_row = moe[:, 0:B, :]
        y_out = moe[:, :, :].rearrange("p (n t) c -> p n t c", n=2)
        g_raw = sb("g_raw", [P, 2, N])
        g_hi = sb("g_hi", [P, FT + 1, N], F32R)
        g_lo = sb("g_lo", [P, FT, N], F32R)
        ident = sb("ident", [P, P])
        ident_r = sb("ident_r", [P, P], F32R)
        w_rows = sb("w_rows", [VP, 2, WCH, C])
        v_col = sb("v_col", [VP, B, VT])
        vb_row = sb("vb_row", [B * VT, VP])
        v_row = sb("v_row", [B * VT, VP])
        p_nat = sb("p_nat", [P, S])
        p_nat_d = sb("p_nat_d", [CR, S])
        q_rows = sb("q_rows", [S, C])
        lu = sb("lu", [S, S])
        bc_row = sb("bc_row", [S, C])
        bc_sq = sb("bc_sq", [S, C])
        bc_scr = sb("bc_scr", [P, C])
        s_small = sb("s_small", [S, 8])
        s_sign = sb("s_sign", [S, S])
        neg_after = sb("neg_after", [S, S])
        u_d = sb("u_d", [S, DW])
        skew = sb("skew", [S, B, S])
        skew_b = sb("skew_b", [S, B, S])
        rs_norm = sb("rs_norm", [S, 2, B])
        pow2 = sb("pow2", [S, SQUARINGS])
        sq_on = sb("sq_on", [S, B, SQUARINGS])
        sq_off = sb("sq_off", [S, B, SQUARINGS])
        sq_tmp = sb("sq_tmp", [S, B, SQUARINGS])
        e_scale = sb("e_scale", [S, B])
        rot = sb("rot", [S, B, 2, S])
        rot_new = sb("rot_new", [S, B, 2, S])
        y_t = sb("y_t", [S, B, C])
        m_hi = sb("m_hi", [P, B, C], F32R)
        m_lo = sb("m_lo", [P, B, C], F32R)
        m_d = sb("m_d", [DW, B, C], F32R)

        v_scratch = nc.dram_tensor("v_scratch", [B * VT, VP], F32, kind="Internal").ap()

        s_banks = [bank(f"s_bank{i}") for i in range(S_BANKS)]
        o_bank = bank("o_bank")
        m_banks = [bank(f"m_bank{i}") for i in range(M_BANKS)]
        d_banks = [bank(f"d_bank{i}") for i in range(D_BANKS)]

        m_drained = [sem(f"m_drained{i}") for i in range(M_BANKS)]
        d_drained = [sem(f"d_drained{i}") for i in range(D_BANKS)]
        x_in = [sem(f"x_in{i}") for i in range(B)]
        c_in = sem("c_in")
        gain_in = sem("gain_in")
        ada_in = sem("ada_in")
        item_in = sem("item_in")
        p_in = sem("p_in")
        w_in = [sem(f"w_in{i}") for i in range(2)]
        scratch_in = sem("scratch_in")
        skew_in = sem("skew_in")
        y_stored = [sem(f"y_stored{i}") for i in range(2)]
        names = ("zeroed ident_ready consts_ready weights_ready c_exp c_wide mods_part mods_full xn_ready "
                 "h_tok_ready h_turned h_hi_ready qkv_full qk_normed hi_ready stack_ready stack_turned scores_full probs_ready "
                 "pv_done o_copied o_turned o_taken max_full max_turned max_placed proj_full "
                 "gate_full gate_shifted gate_exp up_full g_raw_ready g_lo_ready down_full y_ready "
                 "dve_done pool_done solver_full col_done v_summed "
                 "norm_in norm_out rot_ready").split()
        s = {n: sem(n) for n in names}

        def ring_m():
            return Banks(m_banks, m_drained)

        def ring_d():
            return Banks(d_banks, d_drained)

        def layer_dmas(l):
            names_ = [("L0_cond_w_qkv", "L0_cond_b_qkv", "L0_cond_w_proj", "L0_cond_b_proj"),
                      ("L1_cond_w_qkv", "L1_cond_b_qkv", "L1_cond_w_proj", "L1_cond_b_proj"),
                      ("L2_cond_W_qkv", "L2_cond_b_qkv", "L2_cond_W_proj", "L2_cond_b_proj")][l]
            main, d = raw_a[:, :], raw_d[:, :]
            out_ = []
            for w, b, at, n in ((names_[0], names_[1], 0, 3 * C), (names_[2], names_[3], 3 * C, C)):
                out_.append((main[:, at:at + n], a[w][0:P, :]))
                for r in (0, 32, 64):
                    out_.append((d[r:r + CR, at:at + n], a[w][P:C, :]))
                for r in (16, 80):
                    out_.append((d[r:r + 1, at:at + n], a[b].rearrange("(o n) -> o n", o=1)))
            if l == 0:
                out_.append((main[:, GATE_AT:NLG], a["L0_cond_w_gate"][0:P, :]))
                for r in (0, 32, 64):
                    out_.append((d[r:r + CR, NMD:NMD + EXPERTS], a["L0_cond_w_gate"][P:C, :]))
            return out_

        def mlp_dmas(m):
            if m < EXPERTS * B:
                e = m % EXPERTS
                w1, b1 = a["L0_cond_w1"][e], a["L0_cond_b1"][e]
                w2, b2 = a["L0_cond_w2"][e], a["L0_cond_b2"][e]
            elif m < EXPERTS * B + B:
                w1, b1, w2, b2 = (a[f"L1_cond_{n}"] for n in ("w1", "b1", "w2", "b2"))
            else:
                w1, b1, w2, b2 = (a[f"L2_cond_{n}"] for n in ("W_fc1", "b_fc1", "W_fc2", "b_fc2"))
            row = lambda v: v.rearrange("(o n) -> o n", o=1)
            main, d = raw_a[:, :], raw_d[:, :]
            out_ = []
            for at, lo, n in ((0, 0, FF), (FF, FT * P, FR)):
                out_.append((main[:, at:at + n], w1[0:P, lo:lo + n]))
                for r in (0, 32, 64):
                    out_.append((d[r:r + CR, at:at + n], w1[P:C, lo:lo + n]))
                for r in (16, 80):
                    out_.append((d[r:r + 1, at:at + n], row(b1)[:, lo:lo + n]))
            out_.append((main[:, W2_AT:W2T_AT].rearrange("p (f n) -> p f n", f=FT),
                         w2[0:FT * P, :].rearrange("(f p) n -> p f n", p=P)))
            for r in (0, FR):
                out_.append((main[r:r + FR, W2T_AT:NM], w2[FT * P:FF, :]))
            for r in (0, 64):
                out_.append((d[r:r + 1, N1:NMD], row(b2)))
            return out_

        mlp_at = {mlp_item(m): m for m in range(MLPS)}
        item_dmas, staged = [], []
        for i in range(ITEMS):
            item_dmas.append(layer_dmas(LAYER_ITEM.index(i)) if i in LAYER_ITEM else mlp_dmas(mlp_at[i]))
            staged.append(16 * sum(len(dmas) for dmas in item_dmas))

        block = ctx.enter_context(nc.Block())

        @block.sync
        def _(sp):
            def load_item(i):
                if i == 0:
                    sp.wait_ge(s["zeroed"], 1)
                else:
                    sp.wait_ge(s["weights_ready"], i)
                for dst, src in item_dmas[i]:
                    sp.dma_start(dst, src).then_inc(item_in, 16)

            def load_ada(l):
                if l:
                    sp.wait_ge(s["mods_part"], 4 * l)
                w, b = [("L0_cond_w_adaln", "L0_cond_b_adaln"), ("L1_cond_w_mod", "L1_cond_b_mod"),
                        ("L2_cond_W_ada", "L2_cond_b_ada")][l]
                sp.dma_start(ada_a[:, :], a[w][0:P, :]).then_inc(ada_in, 16)
                sp.dma_start(ada_d[0:CR, :], a[w][P:C, :]).then_inc(ada_in, 16)
                sp.dma_start(ada_d[CR:CR + 1, :], a[b].rearrange("(o n) -> o n", o=1)).then_inc(ada_in, 16)

            def load_w(i):
                if i >= 2:
                    sp.wait_ge(s["v_summed"], WCH * (i - 1))
                sp.dma_start(w_rows[:, i % 2, :, :],
                             a["L3_cond_W"].rearrange("(t p) c -> p t c", p=VP)[:, WCH * i:WCH * (i + 1), :])\
                    .then_inc(w_in[i % 2], 16)

            cond = a["cond_1152"]
            sp.dma_start(c_row[:, :, :], cond.rearrange("(o b) c -> o b c", o=1).to_broadcast([P, B, C]))\
                .then_inc(c_in, 16)
            sp.dma_start(c_a[:, :], cond[:, 0:P].rearrange("b c -> c b"), allow_slow_non_contiguous=True)\
                .then_inc(c_in, 16)
            sp.dma_start(c_d[:, :], cond[:, P:C].rearrange("b c -> c b"), allow_slow_non_contiguous=True)\
                .then_inc(c_in, 16)
            load_ada(0)
            for b in range(B):
                sp.dma_start(x_tok[:, b * T:(b + 1) * T, :], a["x"][b].rearrange("(t p) c -> p t c", p=P))\
                    .then_inc(x_in[b], 16)
            load_item(0)
            for b in range(B):
                sp.dma_start(vb_row[b * VT:(b + 1) * VT, :], a["L3_cond_b"].rearrange("(t p) -> t p", p=VP))\
                    .then_inc(p_in, 16)
            sp.dma_start(p_nat[:, :], a["L3_cond_P"][0:P, :]).then_inc(p_in, 16)
            sp.dma_start(p_nat_d[:, :], a["L3_cond_P"][P:C, :]).then_inc(p_in, 16)
            for i, g in enumerate(("L1_cond_g_q", "L1_cond_g_k")):
                sp.dma_start(qk_gain[:, i, :], a[g].rearrange("(o n) -> o n", o=1).to_broadcast([P, HD]))\
                    .then_inc(gain_in, 16)
            load_w(0)
            load_w(1)
            load_ada(1)
            load_item(1)
            for i in range(2, VT // WCH):
                load_w(i)
            load_item(2)
            load_item(3)
            sp.wait_ge(scratch_in, 16)
            sp.wait_ge(s["consts_ready"], 1)
            flat = v_scratch.rearrange("(b t) p -> b (t p)", b=B)
            off = 0
            for i in range(S - 1):
                n = S - 1 - i
                sp.dma_start(skew[i:i + 1, :, i + 1:S], flat[:, off:off + n].rearrange("(o b) n -> o b n", o=1),
                             allow_slow_non_contiguous=(n == 1)).then_inc(skew_in, 16)
                off += n
            for i in range(4, ITEMS):
                if i == mlp_item(EXPERTS + 2):
                    load_ada(2)
                load_item(i)
            for n in range(2 * B):
                b, pair = divmod(n, 2)
                sp.wait_ge(s["y_ready"], n + 1)
                sp.dma_start(out[b].rearrange("(t p) c -> p t c", p=P)[:, 2 * pair:2 * pair + 2, :],
                             y_out[:, n % 2, :, :]).then_inc(y_stored[n % 2], 16)
            for i in range(2):
                sp.wait_ge(y_stored[i], 32)

        @block.gpsimd
        def _(pool):
            ring, mring, seen = ring_d(), ring_m(), Tally()
            done = [0]

            def link(ins):
                done[0] += 1
                ins.then_inc(s["pool_done"], 1)
                pool.wait_ge(s["pool_done"], done[0])

            pool.memset(raw_d[:, :], 0.0).then_inc(s["zeroed"], 1)
            link(pool.memset(ident[:, :], 0.0))
            pool.affine_select(out=ident[:, :], in_=ident[:, :], compare_op=ALU.not_equal, fill=1.0, base=0,
                               pattern=[[-1, P]], channel_multiplier=1).then_inc(s["ident_ready"], 1)
            link(pool.memset(h_tok[:, :, :], 0.0))
            for at in (C, P + 64 + CR):
                link(pool.memset(h_tok[:, :, at:at + 1], 1.0))
            link(pool.memset(qs_tok[:, :, :].bitcast(F32), 0.0))
            link(pool.memset(ks_tok[:, :, :].bitcast(F32), 0.0))
            link(pool.memset(ks_tok[:, :, MAXROW:MAXROW + 1].bitcast(F32), 1.0))
            link(pool.memset(v_aug[:, :, :, :], 1.0))
            link(pool.memset(ones_r[:, :].bitcast(F32), 1.0))
            link(pool.memset(lower[:, :, :], 1.0))
            link(pool.affine_select(out=lower[:, :, :], in_=lower[:, :, :], compare_op=ALU.is_gt, fill=0.0, base=0,
                                    pattern=[[1, EXPERTS], [-1, EXPERTS]], channel_multiplier=0))
            link(pool.memset(neg_after[:, :], -1.0))
            link(pool.affine_select(out=neg_after[:, :], in_=neg_after[:, :], compare_op=ALU.is_gt, fill=0.0, base=0,
                                    pattern=[[-1, S]], channel_multiplier=1))
            link(pool.tensor_copy(ident_r[:, :], ident[:, :]))
            link(pool.memset(row_max[:, :, :, :].bitcast(F32), 0.0))
            link(pool.memset(u_d[:, :], 0.0))
            for i in range(SQUARINGS):
                pool.memset(pow2[:, i:i + 1], float(2 ** i)).then_inc(s["pool_done"], 1)
            done[0] += SQUARINGS
            pool.memset(skew[:, :, :], 0.0).then_inc(s["consts_ready"], 1)

            def prep(i):
                if i in LAYER_ITEM:
                    l = LAYER_ITEM.index(i)
                    na = NLG if l == 0 else NL
                    hi, lo, d = lay_hi[:, l % 2, :], lay_lo[:, l % 2, :], lay_d[:, l % 2, :]
                    cuts = [(0, 0, NL)] + ([(NL, NMD, EXPERTS)] if l == 0 else [])
                    if l == 2:
                        pool.wait_ge(s["gate_full"], B)
                else:
                    m = mlp_at[i]
                    na, cuts = NM, [(0, 0, NMD)]
                    hi, lo, d = ff_hi[:, m % 2, :], ff_lo[:, m % 2, :], ff_d[:, m % 2, :]
                    if m >= 2:
                        pool.wait_ge(s["down_full"], 2 * (m - 1))
                pool.wait_ge(item_in, staged[i])
                link(pool.tensor_copy(hi[:, 0:na], raw_a[:, 0:na]))
                pool.tensor_tensor(lo[:, 0:na], raw_a[:, 0:na], hi[:, 0:na].bitcast(F32), ALU.subtract)\
                    .then_inc(s["pool_done"], 1)
                done[0] += 1
                for to, frm, n in cuts:
                    link(pool.tensor_copy(d[:, to:to + n], raw_d[:, frm:frm + n]))
                for c, (to, frm, n) in enumerate(cuts):
                    ins = pool.tensor_tensor(d[64:DW, to:to + n], raw_d[64:DW, frm:frm + n],
                                             d[64:DW, to:to + n].bitcast(F32), ALU.subtract)
                    if c < len(cuts) - 1:
                        link(ins)
                ins.then_inc(s["weights_ready"], 1)
                pool.wait_ge(s["weights_ready"], i + 1)

            def norm(blk, kind):
                b, l = blk % B, blk // B
                mv = mod[:, b, l % 2, :, :]
                first = 0 if kind == "msa" else 3
                if kind == "o":
                    pool.wait_ge(s["o_taken"], G * (blk + 1))
                    if seen.n.get("norm", 0):
                        pool.wait_ge(s["h_turned"], T * seen.n["norm"])
                seen.next("norm")
                for t in range(T):
                    if kind != "o":
                        pool.wait_ge(s["xn_ready"], seen.next("xn_ready"))
                    tile = h_tok[:, t, 0:C]
                    d2 = h_tok[:, t, P + 32:P + DW].rearrange("p (r w) -> p r w", r=2)[:, :, 0:CR]
                    src = h_tok[:, t, P:C]
                    if kind in ("msa", "mlp"):
                        link(pool.tensor_tensor(tile, tile, mv[:, first + 1, :], ALU.mult))
                        link(pool.tensor_tensor(tile, tile, mv[:, first, :], ALU.add))
                    elif kind == "o":
                        link(pool.tensor_copy(tile, o_tok[:, blk % 2, t, :]))
                    pool.tensor_copy(d2, src.unsqueeze(1).to_broadcast([P, 2, CR]))\
                        .then_inc(s["h_tok_ready"], 1)
                yield
                ring.take(), ring.take()
                yield
                yield

            def qkv(blk):
                for slot in range(2 + T):
                    ring.take(), ring.take()
                    if 1 <= slot <= T:
                        t = slot - 1
                        heads = lambda at: qkv_tok[:, t, at:at + C].rearrange("p (h d) -> p h d", d=HD)
                        pool.wait_ge(s["hi_ready"], 3 * seen.next("hi_ready"))
                        pool.tensor_tensor(qs_tok[:, :, 2 * HD:3 * HD], heads(0), qs_tok[:, :, 0:HD].bitcast(F32),
                                           ALU.subtract).then_inc(s["stack_ready"], 1)
                        pool.tensor_tensor(ks_tok[:, :, HD:2 * HD], heads(C), ks_tok[:, :, 0:HD].bitcast(F32),
                                           ALU.subtract).then_inc(s["stack_ready"], 1)
                    yield

            def mlp(m, blk):
                for slot, banks in enumerate(BANKS_OF["mlp"]):
                    for _ in range(banks):
                        ring.take()
                    if slot == 0 and 1 <= m < MLPS - 1:
                        prep(mlp_item(m + 1))
                    yield

            def solver(step):
                if step[0] in SOLVER_BANK:
                    mring.take()
                if step[0] == "scale":
                    pool.wait_ge(s["norm_in"], 1)
                    pool.partition_all_reduce(rs_norm[:, 1, :], rs_norm[:, 0, :], S, RMAX).then_inc(s["norm_out"], 1)

            walk = {"norm": norm, "qkv": qkv, "mlp": mlp}

            def side(todo):
                for st in todo:
                    if st[0] == "prep":
                        prep(*st[1:])
                    else:
                        yield from walk[st[0]](*st[1:]) if st[0] in walk else idle(ring, st[0])

            for _ in side(HEAD):
                pass
            woven = side(WOVEN)
            for n in range(BLOCKS * STEPS):
                for _ in range(SLOTS[n]):
                    next(woven)
                for part in SOLVER_PLAN[n]:
                    solver(part)
            for _ in side(TAIL):
                pass

        @block.scalar
        def _(act):
            ring, mring, seen = ring_d(), ring_m(), Tally()

            act.wait_ge(c_in, 48)
            act.activation(e_a[:, :], c_a[:, :], ACT.Exp, scale=-1.0).then_inc(s["c_exp"], 1)
            act.activation(e_d[:, :], c_d[:, :], ACT.Exp, scale=-1.0).then_inc(s["c_exp"], 1)
            act.activation(e_row, c_row[:, :, :], ACT.Exp, scale=-1.0).then_inc(s["c_exp"], 1)

            def exps(n):
                if n >= PROBS and n % GRP == 0:
                    act.wait_ge(s["pv_done"], (n - PROBS) // GRP + 1)
                act.wait_ge(s["scores_full"], n + 1)
                act.activation(probs[:, n % PROBS, :], s_banks[n % S_BANKS][:, :], ACT.Exp, scale=HD ** -0.5)\
                    .then_inc(s["probs_ready"], 1)

            def o_copy(grp):
                act.wait_ge(s["pv_done"], T * (grp + 1))
                act.activation(o_t[:, :], o_bank[:, :], ACT.Copy).then_inc(s["o_copied"], 1)

            def norm(blk, kind):
                yield
                (a_bank, _, _), (d_bank, _, _) = ring.take(), ring.take()
                yield
                act.wait_ge(s["h_turned"], T * seen.next("norm"))
                act.activation(h_hi[:, :], a_bank[:, :], ACT.Copy).then_inc(s["h_hi_ready"], 1)
                act.activation(h_d[:, :], d_bank[0:DW, :], ACT.Copy).then_inc(s["h_hi_ready"], 1)
                yield

            def qkv(blk):
                copied = []
                for slot in range(2 + T):
                    taken = ring.take(), ring.take()
                    if slot < 2:
                        copied += [(drained, before + 1) for _, drained, before in taken]
                        for i, (bk, drained, _) in enumerate(taken):
                            act.wait_ge(s["qkv_full"], seen.next("qkv_full"))
                            act.activation(qkv_tok[:, 2 * slot + i, :], bk[:, 0:3 * C], ACT.Copy).then_inc(drained, 1)
                    else:
                        bk, drained, _ = taken[0]
                        act.wait_ge(s["stack_turned"], seen.next("stack_turned"))
                        act.activation(q_t[:, blk % 2, :, (slot - 2) * P:(slot - 1) * P],
                                       bk[:, :].rearrange("p (g n) -> p g n", g=G), ACT.Copy).then_inc(drained, 1)
                        bk, drained, _ = taken[1]
                        act.wait_ge(s["stack_turned"], seen.next("stack_turned"))
                        act.activation(k_t[:, blk % 2, :, (slot - 2) * P:(slot - 1) * P],
                                       bk[:, :].rearrange("p (g n) -> p g n", g=G), ACT.Copy).then_inc(drained, 1)
                    if 1 <= slot <= T:
                        t = slot - 1
                        tile = qkv_tok[:, t, :]
                        heads = lambda at: tile[:, at:at + C].rearrange("p (h d) -> p h d", d=HD)
                        places = lambda to: to[:, :, 0:3 * HD].rearrange("p h (w d) -> p h w d", w=3)
                        if blk // B == 1:
                            act.wait_ge(s["qk_normed"], seen.next("qk_normed"))
                        else:
                            act.wait_ge(*copied[t])
                        if seen.n.get("stack_turned", 0):
                            act.wait_ge(s["stack_turned"], 2 * seen.n.get("stack", 0))
                        seen.next("stack")
                        act.activation(v_aug[:, blk % 2, t, 0:NH * VW].rearrange("p (h w) -> p h w", w=VW)[:, :, 0:HD],
                                       heads(2 * C), ACT.Copy).then_inc(s["hi_ready"], 1)
                        for to, at, w in ((qs_tok, 0, slice(0, 2)), (ks_tok, C, slice(0, 3, 2))):
                            act.activation(places(to)[:, :, w, :],
                                           heads(at).unsqueeze(2).to_broadcast([P, NH, 2, HD]), ACT.Copy)\
                                .then_inc(s["hi_ready"], 1)
                    yield

            def gate(blk):
                ring.take()
                yield
                act.wait_ge(s["gate_shifted"], seen.next("gate_shifted"))
                act.activation(cw[:, :, :], logits[:, :, :], ACT.Exp).then_inc(s["gate_exp"], 1)
                yield

            def mlp(m, blk):
                for f in range(FT + 1):
                    bk, drained, _ = ring.take()
                    n = seen.next("up_full")
                    act.wait_ge(s["up_full"], n)
                    if n > 2:
                        act.wait_ge(s["g_lo_ready"], n - 2)
                    act.activation(g_raw[:, (n - 1) % 2, :], bk[:, :], ACT.Gelu_apprx_tanh)\
                        .then_inc(s["g_raw_ready"], 1)
                    act.activation(g_hi[:, f, :], bk[:, :], ACT.Gelu_apprx_tanh).then_inc(drained, 1)
                ring.take(), ring.take()
                yield
                yield

            def solver(step):
                if step[0] in SOLVER_BANK:
                    bk, drained, before = mring.take()
                    full = seen.next("solver_full")
                if step[0] == "v_rows":
                    act.wait_ge(drained, before + 1)
                    act.dma_start(v_scratch, v_row[:, :]).then_inc(scratch_in, 16)
                elif step[0] == "p_load":
                    act.wait_ge(s["solver_full"], full)
                    act.activation(q_rows[:, :], bk[0:S, 0:C], ACT.Copy).then_inc(drained, 1)

            walk = {"norm": norm, "qkv": qkv, "gate": gate, "mlp": mlp}

            def side(todo):
                for st in todo:
                    yield from walk[st[0]](*st[1:]) if st[0] in walk else idle(ring, st[0])

            for slot, _ in enumerate(side(HEAD)):
                for part in head_parts(slot):
                    solver(part)
            for i in range(T * GRP):
                mring.take()
                for part in first_parts(i):
                    solver(part)
            mring.take()
            woven = side(WOVEN)

            for n in range(BLOCKS * STEPS + 1):
                if n % GSTEPS == 3 and n > GSTEPS:
                    o_copy(n // GSTEPS - 1)
                if n:
                    for _ in range(SLOTS[n - 1]):
                        next(woven)
                    for part in SOLVER_PLAN[n - 1]:
                        solver(part)
                if n < BLOCKS * STEPS:
                    exps(n)
                if n // GSTEPS + 1 < BLOCKS * G:
                    for _ in max_tiles(n):
                        mring.take()
                    if n % GSTEPS == TURN_AT:
                        mring.take()
            o_copy(BLOCKS * G - 1)
            for _ in side(TAIL):
                pass

        @block.vector
        def _(dve):
            ring, mring, seen = ring_d(), ring_m(), Tally()
            done = [0]

            def link(ins):
                done[0] += 1
                ins.then_inc(s["dve_done"], 1)
                dve.wait_ge(s["dve_done"], done[0])

            fill = [lambda: None]

            def rsqrt(y, v, t):
                link(dve.tensor_scalar(y.bitcast(I32), v.bitcast(I32), -0.5, 1597463007.0, ALU.mult, ALU.add))
                for _ in range(3):
                    link(dve.scalar_tensor_tensor(out=t, in0=v, scalar=-0.5, in1=y, op0=ALU.mult, op1=ALU.mult))
                    link(dve.tensor_tensor(t, t, y, ALU.mult))
                    link(dve.scalar_tensor_tensor(out=y, in0=t, scalar=1.5, in1=y, op0=ALU.add, op1=ALU.mult))

            link(dve.memset(c_wide_d[:, :, :], 1.0))
            dve.wait_ge(s["c_exp"], 3)
            for e, c in ((e_a[:, :], c_a[:, :]), (e_d[:, :], c_d[:, :]), (e_row, c_row[:, :, :])):
                link(dve.tensor_scalar(e, e, 1.0, None, ALU.add))
                link(dve.reciprocal(e, e))
                link(dve.tensor_tensor(c, c, e, ALU.mult))
                if c.shape[0] == P and len(c.shape) == 2:
                    dve.tensor_copy(c_wide_a[:, :, :], c_a[:, :].unsqueeze(2).to_broadcast([P, B, P]))\
                        .then_inc(s["c_wide"], 1)
                if c.shape[0] == CR:
                    dve.tensor_copy(c_wide_d[0:CR, :, :], c_d[:, :].unsqueeze(2).to_broadcast([CR, B, P]))\
                        .then_inc(s["c_wide"], 1)

            def take_max(grp, t, j):
                bk, drained, _ = mring.take()
                dve.wait_ge(s["max_full"], seen.next("max_full"))
                dve.tensor_reduce(row_max[:, grp % 2, t, MAXROW + 32 * j:MAXROW + 32 * j + 1], bk[:, :], AX.X, ALU.max).then_inc(drained, 1)

            def place_max(grp):
                bk, drained, before = mring.take()
                q = q_t[:, grp // G % 2, grp % G, :]
                dve.wait_ge(s["max_turned"], grp + 1)
                dve.scalar_tensor_tensor(out=q, in0=bk[:, :], scalar=-1.0, in1=q.bitcast(F32), op0=ALU.mult,
                                         op1=ALU.add).then_inc(drained, 1)
                dve.wait_ge(drained, before + 1)

            def o_normalise(grp):
                dve.wait_ge(s["o_turned"], grp + 1)
                view = o_bank[:, :].rearrange("p (t j w) -> p t j w", t=T, j=GRP)
                link(dve.reciprocal(o_rden[:, :, :], view[:, :, :, HD]))
                g = grp % G
                dst = o_tok[:, grp // G % 2, :, g * GRP * HD:(g + 1) * GRP * HD].rearrange("p t (j d) -> p t j d", d=HD)
                dve.tensor_tensor(dst, view[:, :, :, 0:HD], o_rden[:, :, :].unsqueeze(3).to_broadcast([P, T, GRP, HD]),
                                  ALU.mult).then_inc(s["o_taken"], 1)

            def mods(l, b):
                for half in range(2):
                    bk, drained, before = ring.take()
                    dve.wait_ge(s["mods_full"], seen.next("mods_full"))
                    src = bk[:, 0:3 * C].rearrange("p (v c) -> p v c", v=3)
                    dst = mod[:, b, l % 2, 3 * half:3 * half + 3, :]
                    dve.tensor_copy(dst[:, 0:3:2, :], src[:, 0:3:2, :]).then_inc(s["mods_part"], 1)
                    dve.tensor_scalar(dst[:, 1, :], src[:, 1, :], 1.0, None, ALU.add).then_inc(drained, 1)
                    dve.wait_ge(drained, before + 1)
                    dve.wait_ge(s["mods_part"], seen.next("mods_part"))
                yield

            def norm(blk, kind):
                b = blk % B
                if kind != "o":
                    if kind == "msa" and blk < B:
                        dve.wait_ge(x_in[b], 16)
                    if kind != "x":
                        for i in range(T):
                            dve.bn_stats(stat[:, i, :], x_tok[:, b * T + i, :]).then_inc(s["dve_done"], 1)
                        done[0] += T
                        fill[0]()
                        dve.wait_ge(s["dve_done"], done[0])
                        for i in range(T):
                            dve.bn_aggr(mean_var[:, i, :], stat[:, i, :]).then_inc(s["dve_done"], 1)
                        done[0] += T
                        dve.wait_ge(s["dve_done"], done[0])
                        link(dve.tensor_scalar(nwt[:, 1, 0:T], mean_var[:, :, 1], EPS, None, ALU.add))
                        rsqrt(rstd[:, :], nwt[:, 1, 0:T], nwt[:, 0, 0:T])
                    if seen.n.get("norm", 0):
                        dve.wait_ge(s["h_turned"], T * seen.n["norm"])
                    else:
                        dve.wait_ge(s["consts_ready"], 1)
                    for t in range(T):
                        tile = x_tok[:, b * T + t, :]
                        if kind == "x":
                            ins = dve.tensor_copy(h_tok[:, t, 0:C], tile)
                        else:
                            ins = dve.tensor_scalar(h_tok[:, t, 0:C], tile, mean_var[:, t, 0:1], rstd[:, t:t + 1],
                                                    ALU.subtract, ALU.mult)
                        ins.then_inc(s["xn_ready"], 1)
                seen.next("norm")
                yield
                (a_bank, a_free, _), (d_bank, d_free, _) = ring.take(), ring.take()
                yield
                fill[0]()
                dve.wait_ge(s["h_hi_ready"], 2 * seen.n["norm"] - 1)
                dve.tensor_tensor(h_lo[:, :], a_bank[:, :], h_hi[:, :].bitcast(F32), ALU.subtract)\
                    .then_inc(a_free, 1)
                dve.wait_ge(s["h_hi_ready"], 2 * seen.n["norm"])
                dve.tensor_tensor(h_d[32:64, :], d_bank[32:64, :], h_d[32:64, :].bitcast(F32), ALU.subtract)\
                    .then_inc(d_free, 1)
                yield

            def qkv(blk):
                l, copied = blk // B, []
                for slot in range(2 + T):
                    taken = ring.take(), ring.take()
                    if slot < 2:
                        copied += [(drained, before + 1) for _, drained, before in taken]
                    if slot < T and l == 1:
                        t = slot
                        if blk == B and t == 0:
                            dve.wait_ge(gain_in, 32)
                        dve.wait_ge(*copied[t])
                        qk = qkv_tok[:, t, 0:2 * C].rearrange("p (h d) -> p h d", d=HD)
                        wide = lambda v: v.unsqueeze(2).to_broadcast([P, 2 * NH, HD])
                        dve.tensor_reduce(qk_mean[:, :], qk, AX.X, ALU.add).then_inc(s["dve_done"], 1)
                        done[0] += 1
                        fill[0]()
                        dve.wait_ge(s["dve_done"], done[0])
                        link(dve.tensor_scalar(qk_mean[:, :], qk_mean[:, :], 1.0 / HD, None, ALU.mult))
                        link(dve.tensor_tensor(qk, qk, wide(qk_mean[:, :]), ALU.subtract))
                        link(dve.tensor_tensor(qk_sq[:, :, :], qk, qk, ALU.mult))
                        link(dve.tensor_reduce(qk_var[:, :], qk_sq[:, :, :], AX.X, ALU.add))
                        link(dve.tensor_scalar(qk_var[:, :], qk_var[:, :], 1.0 / HD, EPS, ALU.mult, ALU.add))
                        rsqrt(qk_rstd[:, :], qk_var[:, :], nwt[:, 0, :])
                        link(dve.tensor_tensor(qk, qk, wide(qk_rstd[:, :]), ALU.mult))
                        g4 = qkv_tok[:, t, 0:2 * C].rearrange("p (w h d) -> p w h d", w=2, d=HD)
                        dve.tensor_tensor(g4, g4, qk_gain[:, :, :].unsqueeze(2).to_broadcast([P, 2, NH, HD]),
                                          ALU.mult).then_inc(s["qk_normed"], 1)
                        dve.wait_ge(s["qk_normed"], seen.next("qk_normed"))
                    yield

            def residual(bk, drained, before, blk, t0, vector):
                b, l = blk % B, blk // B
                gv = mod[:, b, l % 2, vector, :].unsqueeze(1).to_broadcast([P, 2, C])
                dve.tensor_tensor(gated[:, :, :], bk[:, 0:2 * C].rearrange("p (t c) -> p t c", t=2), gv, ALU.mult)\
                    .then_inc(drained, 1)
                dve.wait_ge(drained, before + 1)
                xs = x_tok[:, b * T + t0:b * T + t0 + 2, :]
                link(dve.tensor_tensor(xs, xs, gated[:, :, :], ALU.add))

            def proj(blk):
                for pair in range(2):
                    bk, drained, before = ring.take()
                    dve.wait_ge(s["proj_full"], seen.next("proj_full"))
                    residual(bk, drained, before, blk, 2 * pair, 2)
                yield

            def gate(blk):
                bk, drained, before = ring.take()
                dve.wait_ge(s["gate_full"], seen.next("gate_full"))
                dve.tensor_copy(logits[:, :, :], bk[:, 0:T * EXPERTS].rearrange("p (t e) -> p t e", t=T))\
                    .then_inc(drained, 1)
                dve.wait_ge(drained, before + 1)
                e4 = [P, T, EXPERTS, EXPERTS]
                for i, op in ((0, ALU.is_gt), (1, ALU.is_equal)):
                    for t in range(T):
                        link(dve.tensor_tensor(g_cmp[:, i, EXPERTS * t:EXPERTS * t + EXPERTS, :],
                                               logits[:, t, :].unsqueeze(1).to_broadcast([P, EXPERTS, EXPERTS]),
                                               logits[:, t, :].unsqueeze(2).to_broadcast([P, EXPERTS, EXPERTS]), op))
                eq = g_cmp[:, 1, :, :].rearrange("p (t e) j -> p t e j", t=T)
                link(dve.tensor_tensor(eq, eq, lower[:, :, :].unsqueeze(1).to_broadcast(e4), ALU.mult))
                link(dve.tensor_tensor(g_cmp[:, 0, :, :], g_cmp[:, 0, :, :], g_cmp[:, 1, :, :], ALU.add))
                link(dve.tensor_reduce(g_rank[:, :, :].rearrange("p t e -> p (t e)"), g_cmp[:, 0, :, :], AX.X, ALU.add))
                link(dve.tensor_scalar(g_rank[:, :, :], g_rank[:, :, :], TOP_K - 0.5, None, ALU.is_lt))
                link(dve.tensor_reduce(g_sum[:, :], logits[:, :, :], AX.X, ALU.max))
                dve.tensor_tensor(logits[:, :, :], logits[:, :, :],
                                  g_sum[:, :].unsqueeze(2).to_broadcast([P, T, EXPERTS]), ALU.subtract)\
                    .then_inc(s["gate_shifted"], 1)
                yield
                dve.wait_ge(s["gate_exp"], seen.next("gate_exp"))
                link(dve.tensor_tensor(cw[:, :, :], cw[:, :, :], g_rank[:, :, :], ALU.mult))
                link(dve.tensor_reduce(g_sum[:, :], cw[:, :, :], AX.X, ALU.add))
                link(dve.reciprocal(g_sum[:, :], g_sum[:, :]))
                link(dve.tensor_tensor(cw[:, :, :], cw[:, :, :],
                                       g_sum[:, :].unsqueeze(2).to_broadcast([P, T, EXPERTS]), ALU.mult))
                yield

            def mlp(m, blk):
                for f in range(FT + 1):
                    _, drained, before = ring.take()
                    n = seen.next("g_raw_ready")
                    dve.wait_ge(drained, before + 1)
                    if f < FT:
                        dve.tensor_tensor(g_lo[:, f, :], g_raw[:, (n - 1) % 2, :], g_hi[:, f, :].bitcast(F32),
                                          ALU.subtract).then_inc(s["g_lo_ready"], 1)
                    else:
                        dve.tensor_tensor(g_hi[FR:P, f, :], g_raw[FR:P, (n - 1) % 2, :],
                                          g_hi[FR:P, f, :].bitcast(F32), ALU.subtract)\
                            .then_inc(s["g_lo_ready"], 1)
                down = ring.take(), ring.take()
                yield
                for pair, (bk, drained, before) in enumerate(down):
                    dve.wait_ge(s["down_full"], seen.next("down_full"))
                    if blk // B == 0:
                        e = m % EXPERTS
                        for i in range(2):
                            t = 2 * pair + i
                            src, w = bk[:, i * C:(i + 1) * C], cw[:, t, e:e + 1]
                            if e == 0:
                                ins = dve.tensor_scalar(moe[:, t, :], src, w, None, ALU.mult)
                            else:
                                ins = dve.scalar_tensor_tensor(out=moe[:, t, :], in0=src, scalar=w,
                                                               in1=moe[:, t, :], op0=ALU.mult, op1=ALU.add)
                            if i == 0:
                                link(ins)
                        ins.then_inc(drained, 1)
                        dve.wait_ge(drained, before + 1)
                    else:
                        residual(bk, drained, before, blk, 2 * pair, 5)
                    if blk // B == 0 and e == EXPERTS - 1 and pair == 1:
                        b, l = blk % B, blk // B
                        gv = mod[:, b, l % 2, 5, :].unsqueeze(1).to_broadcast([P, T, C])
                        link(dve.tensor_tensor(moe[:, :, :], moe[:, :, :], gv, ALU.mult))
                        xs = x_tok[:, b * T:(b + 1) * T, :]
                        link(dve.tensor_tensor(xs, xs, moe[:, :, :], ALU.add))
                yield

            def rotate(b):
                for pair in range(2):
                    n = 2 * b + pair
                    bk, drained, before = ring.take()
                    dve.wait_ge(s["proj_full"], seen.next("proj_full"))
                    dve.tensor_copy(gated[:, :, :], bk[:, 0:2 * C].rearrange("p (t c) -> p t c", t=2))\
                        .then_inc(drained, 1)
                    dve.wait_ge(drained, before + 1)
                    if n >= 2:
                        dve.wait_ge(y_stored[n % 2], 16)
                    t0 = b * T + 2 * pair
                    dve.tensor_tensor(y_out[:, n % 2, :, :], gated[:, :, :], x_tok[:, t0:t0 + 2, :], ALU.add)\
                        .then_inc(s["y_ready"], 1)
                    dve.wait_ge(s["y_ready"], n + 1)
                yield

            eye = ident[0:S, 0:S]
            eyes = eye.unsqueeze(1).to_broadcast([S, B, S])

            def solver(step, taken):
                kind = step[0]
                if taken:
                    bk, drained, before = taken
                    full = seen.next("solver_full")

                def drain(ins):
                    ins.then_inc(drained, 1)
                    dve.wait_ge(drained, before + 1)

                if kind == "v":
                    t = step[1]
                    i = t // WCH
                    dve.wait_ge(w_in[i % 2], 16 * (i // 2 + 1))
                    for b in range(B):
                        ins = dve.tensor_tensor_reduce(out=bc_scr[0:VP, :], in0=w_rows[:, i % 2, t % WCH, :],
                                                       in1=c_row[0:VP, b, :], scale=1.0, scalar=0.0, op0=ALU.mult,
                                                       op1=ALU.add, accum_out=v_col[:, b, t:t + 1])
                        if b == 0:
                            link(ins)
                    ins.then_inc(s["v_summed"], 1)
                    dve.wait_ge(s["v_summed"], t + 1)
                elif kind == "v_rows":
                    dve.wait_ge(s["solver_full"], full)
                    dve.wait_ge(p_in, 64)
                    dve.tensor_tensor(v_row[:, :], bk[0:B * VT, 0:VP], vb_row[:, :], ALU.add).then_inc(drained, 1)
                elif kind == "mgs":
                    j = step[1]
                    row = bk[0:S, 0:C]
                    dve.wait_ge(s["solver_full"], full)
                    link(dve.tensor_copy(bc_row[:, :], row))
                    dve.tensor_tensor_reduce(out=bc_sq[:, :], in0=bc_row[:, :], in1=bc_row[:, :], scale=1.0, scalar=0.0,
                                             op0=ALU.mult, op1=ALU.add, accum_out=s_small[:, 3:4])\
                        .then_inc(s["dve_done"], 1)
                    dve.tensor_tensor_reduce(out=bc_scr[0:S, :], in0=q_rows[:, :], in1=bc_row[:, :], scale=1.0,
                                             scalar=0.0, op0=ALU.mult, op1=ALU.add, accum_out=s_small[:, 0:1])\
                        .then_inc(s["dve_done"], 1)
                    done[0] += 2
                    fill[0]()
                    dve.wait_ge(s["dve_done"], done[0])
                    link(dve.reciprocal(s_small[:, 1:2], s_small[:, 3:4]))
                    link(dve.tensor_scalar(s_small[:, 2:3], s_small[:, 0:1], s_small[:, 1:2], neg_after[:, j:j + 1],
                                           ALU.mult, ALU.mult))
                    drain(dve.scalar_tensor_tensor(out=q_rows[:, :], in0=bc_row[:, :], scalar=s_small[:, 2:3],
                                                   in1=q_rows[:, :], op0=ALU.mult, op1=ALU.add))
                elif kind == "unit_cols":
                    link(dve.tensor_tensor_reduce(out=bc_scr[0:S, :], in0=q_rows[:, :], in1=q_rows[:, :], scale=1.0,
                                                  scalar=0.0, op0=ALU.mult, op1=ALU.add,
                                                  accum_out=s_small[:, 0:1]))
                    rsqrt(s_small[:, 1:2], s_small[:, 0:1], s_small[:, 2:3])
                    link(dve.tensor_scalar(q_rows[:, :], q_rows[:, :], s_small[:, 1:2], None, ALU.mult))
                    dve.tensor_copy(lu[:, :], q_rows[:, 0:S]).then_inc(s["col_done"], 1)
                elif kind == "lu":
                    j = step[1]
                    dve.wait_ge(s["solver_full"], full)
                    w = bk[0:S, j:j + 1]
                    link(dve.tensor_scalar(s_sign[:, j:j + 1], w, 0.0, 2.0, ALU.is_ge, ALU.mult))
                    dve.scalar_tensor_tensor(out=s_small[:, 0:1], in0=s_sign[:, j:j + 1], scalar=-1.0, in1=w,
                                             op0=ALU.add, op1=ALU.add).then_inc(s["dve_done"], 1)
                    done[0] += 1
                    fill[0]()
                    dve.wait_ge(s["dve_done"], done[0])
                    link(dve.reciprocal(s_small[:, 1:2], s_small[:, 0:1]))
                    link(dve.tensor_scalar(s_small[:, 2:3], lu[:, j:j + 1], s_small[:, 1:2], neg_after[:, j:j + 1],
                                           ALU.mult, ALU.mult))
                    drain(dve.scalar_tensor_tensor(out=lu[:, :], in0=bk[0:S, 0:S], scalar=s_small[:, 2:3],
                                                   in1=lu[:, :], op0=ALU.mult, op1=ALU.add))
                elif kind == "signs":
                    link(dve.tensor_tensor_reduce(out=bc_scr[0:S, 0:S], in0=s_sign[:, :], in1=eye, scale=1.0,
                                                  scalar=0.0, op0=ALU.mult, op1=ALU.add,
                                                  accum_out=s_small[:, 0:1]))
                    link(dve.tensor_scalar(s_small[:, 1:2], s_small[:, 0:1], -1.0, 1.0, ALU.mult, ALU.add))
                    link(dve.tensor_scalar(q_rows[:, :], q_rows[:, :], s_small[:, 1:2], None, ALU.mult))
                    link(dve.tensor_copy(u_d[:, :].rearrange("p (r w) -> p r w", r=3)[:, :, 0:CR],
                                         q_rows[:, P:C].unsqueeze(1).to_broadcast([S, 3, CR])))
                elif kind == "skew":
                    dve.wait_ge(s["solver_full"], full)
                    drain(dve.tensor_tensor(skew_b[:, :, :], skew[:, :, :],
                                            bk[0:S, 0:B * S].rearrange("p (b n) -> p b n", b=B), ALU.subtract))
                    link(dve.scalar_tensor_tensor(out=rot_new[:, :, 0, :], in0=skew_b[:, :, :], scalar=-1.0,
                                                  in1=skew_b[:, :, :], op0=ALU.mult, op1=ALU.max))
                    dve.tensor_reduce(rs_norm[:, 0, :], rot_new[:, :, 0, :], AX.X, ALU.add)\
                        .then_inc(s["norm_in"], 1)
                elif kind == "scale":
                    dve.wait_ge(s["norm_out"], 1)
                    wide = [S, B, SQUARINGS]
                    powers = pow2[:, :].unsqueeze(1).to_broadcast(wide)
                    link(dve.tensor_tensor(sq_on[:, :, :], rs_norm[:, 1, :].unsqueeze(2).to_broadcast(wide), powers,
                                           ALU.is_gt))
                    link(dve.tensor_scalar(sq_off[:, :, :], sq_on[:, :, :], -1.0, 1.0, ALU.mult, ALU.add))
                    link(dve.tensor_tensor(sq_tmp[:, :, :], sq_on[:, :, :], powers, ALU.mult))
                    link(dve.tensor_reduce(e_scale[:, :], sq_tmp[:, :, :], AX.X, ALU.add))
                    link(dve.tensor_scalar(e_scale[:, :], e_scale[:, :], 1.0, None, ALU.add))
                    link(dve.reciprocal(e_scale[:, :], e_scale[:, :]))
                    for b in range(B):
                        link(dve.tensor_scalar(skew_b[:, b, :], skew_b[:, b, :], e_scale[:, b:b + 1], -1.0,
                                               ALU.mult, ALU.mult))
                    dve.scalar_tensor_tensor(out=rot[:, :, 0, :], in0=skew_b[:, :, :], scalar=-1.0 / TAYLOR,
                                             in1=eyes, op0=ALU.mult, op1=ALU.add).then_inc(s["rot_ready"], 1)
                elif kind == "taylor":
                    dve.wait_ge(s["solver_full"], full)
                    drain(dve.scalar_tensor_tensor(out=rot[:, :, 0, :],
                                                   in0=bk[0:S, 0:B * S].rearrange("p (b n) -> p b n", b=B),
                                                   scalar=1.0 / step[1], in1=eyes, op0=ALU.mult, op1=ALU.add))
                elif kind == "turned":
                    dve.wait_ge(s["solver_full"], full)
                    drain(dve.tensor_copy(rot[:, :, 1, :], bk[0:S, 0:B * S].rearrange("p (b n) -> p b n", b=B)))
                elif kind == "square":
                    i = step[1]
                    dve.wait_ge(s["solver_full"], full)
                    flat = lambda v: v.rearrange("p b r n -> p b (r n)")
                    on, off = (v[:, :, i:i + 1].to_broadcast([S, B, 2 * S]) for v in (sq_on, sq_off))
                    link(dve.tensor_tensor(flat(rot_new[:, :, :, :]),
                                           bk[0:S, 0:2 * B * S].rearrange("p (b n) -> p b n", b=B), on, ALU.mult))
                    link(dve.tensor_tensor(flat(rot[:, :, :, :]), flat(rot[:, :, :, :]), off, ALU.mult))
                    drain(dve.tensor_tensor(flat(rot[:, :, :, :]), flat(rot[:, :, :, :]),
                                            flat(rot_new[:, :, :, :]), ALU.add))
                elif kind == "less_one":
                    dve.tensor_tensor(rot[:, :, 1, :], rot[:, :, 1, :], eyes, ALU.subtract)\
                        .then_inc(s["rot_ready"], 1)
                elif kind == "y":
                    dve.wait_ge(s["solver_full"], full)
                    drain(dve.tensor_copy(y_t[:, :, :], bk[0:S, 0:B * C].rearrange("p (b n) -> p b n", b=B)))
                elif kind == "m":
                    b = step[1]
                    dve.wait_ge(s["solver_full"], full)
                    link(dve.tensor_copy(m_hi[:, b, :], bk[:, 0:C]))
                    link(dve.tensor_tensor(m_lo[:, b, :], bk[:, 0:C], m_hi[:, b, :].bitcast(F32), ALU.subtract))
                    link(dve.tensor_copy(m_d[:, b, :], bk[0:DW, 256:256 + C]))
                    drain(dve.tensor_tensor(m_d[64:DW, b, :], bk[64:DW, 256:256 + C],
                                            m_d[64:DW, b, :].bitcast(F32), ALU.subtract))

            walk = {"mods": mods, "norm": norm, "qkv": qkv, "proj": proj, "gate": gate, "mlp": mlp,
                    "rotate": rotate}

            def side(todo):
                for st in todo:
                    yield from walk[st[0]](*st[1:]) if st[0] in walk else idle(ring, st[0])

            def solve(part):
                solver(part, mring.take() if part[0] in SOLVER_BANK else None)

            for slot, _ in enumerate(side(HEAD)):
                for part in head_parts(slot):
                    solve(part)
            for i in range(T * GRP):
                take_max(0, *divmod(i, GRP))
                for part in first_parts(i):
                    solve(part)
            place_max(0)
            woven = side(WOVEN)

            for n in range(BLOCKS * STEPS + 1):
                grp = n // GSTEPS
                if n % GSTEPS == 5 and grp > 0:
                    o_normalise(grp - 1)
                maxima = list(max_tiles(n)) if grp + 1 < BLOCKS * G else []

                def next_max():
                    if maxima:
                        take_max(grp + 1, *maxima.pop(0))

                def fill_once():
                    if len(maxima) == len(max_tiles(n)):
                        next_max()

                if n:
                    taken = [mring.take() if part[0] in SOLVER_BANK else None for part in SOLVER_PLAN[n - 1]]
                    fill[0] = fill_once
                    for _ in range(SLOTS[n - 1]):
                        next(woven)
                    for part, banks in zip(SOLVER_PLAN[n - 1], taken):
                        solver(part, banks)
                    fill[0] = lambda: None
                while maxima:
                    next_max()
                if n % GSTEPS == TURN_AT and grp + 1 < BLOCKS * G:
                    place_max(grp + 1)
            o_normalise(BLOCKS * G - 1)
            for _ in side(TAIL):
                pass

        @block.tensor
        def _(pe):
            ring, mring, seen = ring_d(), ring_m(), Tally()
            placed = {}
            stacks = {}
            h_ready = []

            def take(r):
                bk, drained, before = r.take()
                if before:
                    pe.wait_ge(drained, before)
                return bk, (drained, before + 1)

            def linear(dst, h, w_hi, w_lo, w_d):
                h1, h2, hd = h
                pe.matmul(dst, h1, w_hi, start=True, stop=False)
                pe.matmul(dst, h2, w_hi, start=False, stop=False)
                pe.matmul(dst, h1, w_lo, start=False, stop=False)
                return pe.matmul(dst, hd, w_d, start=False, stop=True)

            def h_tile(t):
                cols = slice(t * P, (t + 1) * P)
                return h_hi[:, cols], h_lo[:, cols], h_d[:, cols]

            def scores(n):
                grp, kt, j = n // GSTEPS, n % GSTEPS // GRP, n % GRP
                par, g = grp // G % 2, grp % G
                rows = slice(32 * j, 32 * j + 32)
                if n % GSTEPS == 0:
                    pe.wait_ge(*placed[grp])
                if n >= S_BANKS:
                    pe.wait_ge(s["probs_ready"], n - S_BANKS + 1)
                pe.matmul(s_banks[n % S_BANKS][:, :], k_t[rows, par, g, kt * P:(kt + 1) * P], q_t[rows, par, g, :],
                          start=True, stop=True).then_inc(s["scores_full"], 1)

            def max_scores(grp, t, j):
                par, g = grp // G % 2, grp % G
                rows = slice(32 * j, 32 * j + 32)
                if grp % G == 0 and t == 0 and j == 0:
                    for w in stacks[grp // G]:
                        pe.wait_ge(*w)
                bk, _ = take(mring)
                pe.matmul(bk[:, :], q_t[rows, par, g, t * P:(t + 1) * P], k_t[rows, par, g, :],
                          start=True, stop=True).then_inc(s["max_full"], 1)

            def max_turn(grp):
                for i in range(M_BANKS):
                    pe.wait_ge(m_drained[i], (mring.n + M_BANKS - 1 - i) // M_BANKS)
                bk, placed[grp] = take(mring)
                for t in range(T):
                    ins = pe.matmul(bk[:, t * P:(t + 1) * P], row_max[:, grp % 2, t, :], ident_r[:, :],
                                    start=True, stop=True)
                ins.then_inc(s["max_turned"], 1)

            def pv(quad):
                grp, kt = quad // T, quad % T
                par, g = grp // G % 2, grp % G
                pe.wait_ge(s["probs_ready"], GRP * (quad + 1))
                if kt == 0 and grp > 0:
                    pe.wait_ge(s["o_taken"], grp)
                for j in range(GRP):
                    at = (g * GRP + j) * VW
                    ins = pe.matmul(o_bank[32 * j:32 * j + 32, :], v_aug[:, par, kt, at:at + 32],
                                    probs[:, (GRP * quad + j) % PROBS, :],
                                    start=(kt == 0), stop=(kt == T - 1), skip_group_check=True)
                ins.then_inc(s["pv_done"], 1)

            def o_turn(grp):
                pe.wait_ge(s["o_copied"], grp + 1)
                for t in range(T):
                    ins = pe.transpose(o_bank[:, t * P:(t + 1) * P], o_t[:, t * P:(t + 1) * P], ident[:, :])
                ins.then_inc(s["o_turned"], 1)

            def mods(l, b):
                for half in range(2):
                    bk, _ = take(ring)
                    pe.wait_ge(ada_in, 48 * (l + 1))
                    pe.wait_ge(s["c_wide"], 2)
                    cols = slice(3 * C * half, 3 * C * (half + 1))
                    pe.matmul(bk[:, 0:3 * C], c_wide_a[:, b, :], ada_a[:, cols], start=True, stop=False)
                    pe.matmul(bk[:, 0:3 * C], c_wide_d[:, b, :], ada_d[:, cols], start=False, stop=True)\
                        .then_inc(s["mods_full"], 1)
                yield

            def norm(blk, kind):
                yield
                (a_bank, a_done), (d_bank, d_done) = take(ring), take(ring)
                if not h_ready:
                    pe.wait_ge(s["ident_ready"], 1)
                    pe.wait_ge(s["consts_ready"], 1)
                for t in range(T):
                    n = seen.next("h_tok_ready")
                    pe.wait_ge(s["h_tok_ready"], n)
                    cols = slice(t * P, (t + 1) * P)
                    pe.transpose(a_bank[:, cols], h_tok[:, t, 0:P], ident[:, :])
                    pe.transpose(d_bank[0:DW, cols], h_tok[:, t, P:P + DW], ident[:, :]).then_inc(s["h_turned"], 1)
                    if t == 1:
                        yield
                h_ready[:] = [a_done, d_done]
                yield

            def h_wait():
                for w in h_ready:
                    pe.wait_ge(*w)

            def qkv(blk):
                l = blk // B
                stacks[blk] = []
                for slot in range(2 + T):
                    if slot < 2:
                        for t in (2 * slot, 2 * slot + 1):
                            bk, _ = take(ring)
                            if t == 0:
                                h_wait()
                                pe.wait_ge(s["weights_ready"], LAYER_ITEM[l] + 1)
                            linear(bk[:, 0:3 * C], h_tile(t), lay_hi[:, l % 2, 0:3 * C], lay_lo[:, l % 2, 0:3 * C],
                                   lay_d[:, l % 2, 0:3 * C]).then_inc(s["qkv_full"], 1)
                    else:
                        (qb, q_done), (kb, k_done) = take(ring), take(ring)
                        seen.next("stack_ready")
                        pe.wait_ge(s["stack_ready"], seen.next("stack_ready"))
                        for bk, src in ((qb, qs_tok), (kb, ks_tok)):
                            for g in range(G):
                                ins = pe.matmul(bk[:, g * P:(g + 1) * P],
                                                src[:, g * GRP:(g + 1) * GRP, :].rearrange("p h w -> p (h w)"),
                                                ident_r[:, :], start=True, stop=True)
                            ins.then_inc(s["stack_turned"], 1)
                        stacks[blk] += [q_done, k_done]
                    yield

            def pair_linear(bk, pair, parts, signal):
                for i in range(2):
                    ins = linear(bk[:, i * C:(i + 1) * C], h_tile(2 * pair + i), *parts)
                ins.then_inc(signal, 1)

            def proj(blk):
                l = blk // B
                cols = slice(3 * C, 4 * C)
                for pair in range(2):
                    bk, _ = take(ring)
                    h_wait()
                    pair_linear(bk, pair, (lay_hi[:, l % 2, cols], lay_lo[:, l % 2, cols], lay_d[:, l % 2, cols]),
                                s["proj_full"])
                yield

            def gate(blk):
                bk, _ = take(ring)
                h_wait()
                cols = slice(GATE_AT, NLG)
                for t in range(T):
                    ins = linear(bk[:, t * EXPERTS:(t + 1) * EXPERTS], h_tile(t), lay_hi[:, 0, cols],
                                 lay_lo[:, 0, cols], lay_d[:, 0, cols])
                ins.then_inc(s["gate_full"], 1)
                yield
                yield

            def mlp(m, blk):
                i = m % 2
                for f in range(FT + 1):
                    bk, _ = take(ring)
                    if f == 0:
                        h_wait()
                        pe.wait_ge(s["weights_ready"], mlp_item(m) + 1)
                    c = slice(f * P, (f + 1) * P)
                    pe.matmul(bk[:, :], ff_hi[:, i, c], h_hi[:, :], start=True, stop=False)
                    pe.matmul(bk[:, :], ff_hi[:, i, c], h_lo[:, :], start=False, stop=False)
                    pe.matmul(bk[:, :], ff_lo[:, i, c], h_hi[:, :], start=False, stop=False)
                    pe.matmul(bk[:, :], ff_d[:, i, c], h_d[:, :], start=False, stop=True)\
                        .then_inc(s["up_full"], 1)
                banks = {}

                def full_rows(t):
                    dst, cols = banks[t // 2][:, t % 2 * C:(t % 2 + 1) * C], slice(t * P, (t + 1) * P)
                    for f in range(FT):
                        if t == 0:
                            pe.wait_ge(s["g_lo_ready"], (FT + 1) * m + f + 1)
                        w = slice(W2_AT + f * C, W2_AT + (f + 1) * C)
                        pe.matmul(dst, g_hi[:, f, cols], ff_hi[:, i, w], start=(f == 0), stop=False)
                        pe.matmul(dst, g_lo[:, f, cols], ff_hi[:, i, w], start=False, stop=False)
                        pe.matmul(dst, g_hi[:, f, cols], ff_lo[:, i, w], start=False, stop=False)

                def last_rows(t):
                    dst, cols = banks[t // 2][:, t % 2 * C:(t % 2 + 1) * C], slice(t * P, (t + 1) * P)
                    w = slice(W2T_AT, NM)
                    pe.matmul(dst, g_hi[:, FT, cols], ff_hi[:, i, w], start=False, stop=False)
                    pe.matmul(dst, g_hi[0:FR, FT, cols], ff_lo[0:FR, i, w], start=False, stop=False)
                    return pe.matmul(dst, ones_r[:, :], ff_d[:, i, N1:NMD], start=False, stop=True)

                banks[0], _ = take(ring)
                full_rows(0)
                banks[1], _ = take(ring)
                full_rows(2)
                pe.wait_ge(s["g_lo_ready"], (FT + 1) * (m + 1))
                last_rows(0)
                full_rows(1)
                last_rows(1).then_inc(s["down_full"], 1)
                last_rows(2)
                full_rows(3)
                last_rows(3).then_inc(s["down_full"], 1)
                yield
                yield

            def rotate(b):
                for pair in range(2):
                    bk, _ = take(ring)
                    h_wait()
                    pe.wait_ge(*m_ready[b])
                    pair_linear(bk, pair, (m_hi[:, b, :], m_lo[:, b, :], m_d[:, b, :]), s["proj_full"])
                yield

            m_ready = {}
            last = [None] * 3

            def solver(step):
                kind = step[0]
                if kind not in SOLVER_BANK:
                    return
                bk, ready = take(mring)
                chain = 0 if step in QR_CHAIN else 1 if step in EXP_CHAIN else 2
                if kind == "v_rows":
                    pe.wait_ge(s["v_summed"], VT)
                    ins = pe.transpose(bk[0:B * VT, 0:VP], v_col[:, :, :].rearrange("p b t -> p (b t)"),
                                       ident[0:VP, 0:VP])
                elif kind == "p_load":
                    pe.wait_ge(p_in, 64)
                    pe.transpose(bk[0:S, 0:P], p_nat[:, :], ident[:, :])
                    ins = pe.transpose(bk[0:S, P:C], p_nat_d[:, :], ident[0:CR, 0:CR])
                elif kind in ("mgs", "lu"):
                    j = step[1]
                    src = q_rows[:, :] if kind == "mgs" else lu[:, :]
                    if kind == "lu" and j == 0:
                        pe.wait_ge(s["col_done"], 1)
                    else:
                        pe.wait_ge(*last[chain])
                    ins = pe.matmul(bk[0:S, 0:src.shape[1]], ident[0:S, j:j + 1].to_broadcast([S, S]), src,
                                    start=True, stop=True)
                elif kind == "skew":
                    pe.wait_ge(skew_in, 16 * (S - 1))
                    for b in range(B):
                        ins = pe.transpose(bk[0:S, b * S:(b + 1) * S], skew[:, b, :], ident[0:S, 0:S])
                elif kind == "taylor":
                    if step[1] == TAYLOR - 1:
                        pe.wait_ge(s["rot_ready"], 1)
                    else:
                        pe.wait_ge(*last[chain])
                    for b in range(B):
                        ins = pe.matmul(bk[0:S, b * S:(b + 1) * S], skew_b[:, b, :], rot[:, b, 0, :],
                                        start=True, stop=True)
                elif kind == "turned":
                    pe.wait_ge(*last[chain])
                    for b in range(B):
                        ins = pe.transpose(bk[0:S, b * S:(b + 1) * S], rot[:, b, 0, :], ident[0:S, 0:S])
                elif kind == "square":
                    pe.wait_ge(*last[chain])
                    for b in range(B):
                        for r in range(2):
                            at = (2 * b + r) * S
                            ins = pe.matmul(bk[0:S, at:at + S], rot[:, b, 1 - r, :], rot[:, b, r, :],
                                            start=True, stop=True)
                elif kind == "y":
                    pe.wait_ge(s["rot_ready"], 2)
                    for b in range(B):
                        ins = pe.matmul(bk[0:S, b * C:(b + 1) * C], rot[:, b, 1, :], q_rows[:, :],
                                        start=True, stop=True)
                elif kind == "m":
                    b = step[1]
                    if b == 0:
                        pe.wait_ge(*last[chain])
                    pe.matmul(bk[:, 0:C], q_rows[:, 0:P], y_t[:, b, :], start=True, stop=True)
                    ins = pe.matmul(bk[0:DW, 256:256 + C], u_d[:, :], y_t[:, b, :], start=True, stop=True)
                    m_ready[b] = ready
                ins.then_inc(s["solver_full"], 1)
                last[chain] = ready

            walk = {"mods": mods, "norm": norm, "qkv": qkv, "proj": proj, "gate": gate, "mlp": mlp,
                    "rotate": rotate}

            def side(todo):
                for st in todo:
                    yield from walk[st[0]](*st[1:]) if st[0] in walk else idle(ring, st[0])

            for slot, _ in enumerate(side(HEAD)):
                for part in head_parts(slot):
                    solver(part)
            for i in range(T * GRP):
                max_scores(0, *divmod(i, GRP))
                for part in first_parts(i):
                    solver(part)
            max_turn(0)
            woven = side(WOVEN)
            for n in range(BLOCKS * STEPS):
                grp = n // GSTEPS
                if grp + 1 < BLOCKS * G:
                    for t, j in max_tiles(n):
                        max_scores(grp + 1, t, j)
                scores(n)
                if n % GSTEPS == 4 and grp > 0:
                    o_turn(grp - 1)
                if n % GRP == 2 and n > GRP:
                    pv(n // GRP - 1)
                if n % GSTEPS == TURN_AT and grp + 1 < BLOCKS * G:
                    max_turn(grp + 1)
                for _ in range(SLOTS[n]):
                    next(woven)
                for part in SOLVER_PLAN[n]:
                    solver(part)
            pv(T * BLOCKS * G - 1)
            o_turn(BLOCKS * G - 1)
            for _ in side(TAIL):
                pass


def kernel(**inputs):
    import numpy as _np
    import concourse.bacc as _bacc
    from concourse.bass_utils import run_bass_kernel_spmd as _run

    nc = _bacc.Bacc("TRN2", target_bir_lowering=False, num_devices=1)
    arrays, args = {}, {}
    for name, value in inputs.items():
        v = _np.ascontiguousarray(value)
        arrays[f"in_{name}_dram"] = v
        args[name] = nc.dram_tensor(f"in_{name}_dram", v.shape, mybir.dt.from_np(v.dtype), kind="ExternalInput").ap()
    out = nc.dram_tensor("out_0_dram", (B, N, C), F32, kind="ExternalOutput").ap()
    build(nc, args, out)
    r = _run(nc, [arrays], core_ids=[0])
    return r.results[0]["out_0_dram"]
```
